# Optimizing a Trainium2 kernel written in Bass

```python
import numpy as np
import jax
import jax.numpy as jnp

def _softmax(x, axis=-1):
    return jax.nn.softmax(x, axis=axis)

def _gelu(x):
    return jax.nn.gelu(x, approximate=True)

def _silu(x):
    return jax.nn.silu(x)

def _sigmoid(x):
    return jax.nn.sigmoid(x)

def _layernorm(x, axis=-1, eps=1e-05):
    m = jnp.mean(x, axis=axis, keepdims=True)
    v = jnp.var(x, axis=axis, keepdims=True)
    return (x - m) / jnp.sqrt(v + eps)

def _scatter_add(tgt, idx, src, axis=0):
    return tgt.at[idx].add(src)

def _segment_sum(src, seg, n):
    return jax.ops.segment_sum(src, seg, n)
kernel_name = 'mk_adaln_d1_jaxref_r4_8fd093'

def setup_inputs(seed: int=0):
    np.random.seed(seed)
    _w = jnp.asarray

    def _L0_attn_setup():
        import jax, jax.numpy as jnp
        import numpy as np
        import math
        B, T, C = (2, 512, 256)
        H, L = (16, 64)
        DH = C // H
        DHE = DH // 2
        THETA = 10000.0

        def _rope_cache(t, dim):
            inv_freq = 1.0 / THETA ** (jnp.arange(0, dim, 2, dtype=jnp.float32) / dim)
            freqs = jnp.arange(t, dtype=jnp.float32)[:, None] * inv_freq[None, :]
            emb = jnp.concatenate((freqs, freqs), axis=-1)
            return (jnp.cos(emb), jnp.sin(emb))

        def _apply_rope(x, cos, sin):
            x1 = x[..., 0::2]
            x2 = x[..., 1::2]
            rot = jnp.stack((-x2, x1), axis=-1).reshape(x.shape)
            return x * cos[None, None] + rot * sin[None, None]
        key = jax.random.key(seed)
        ks = jax.random.split(key, 10)
        s = 0.02
        return {'x': jax.random.normal(ks[0], (B, T, C), jnp.float32), 'Wq_down': jax.random.normal(ks[1], (C, H * L), jnp.float32) * s, 'Wk_down': jax.random.normal(ks[2], (C, H * L), jnp.float32) * s, 'Wv_down': jax.random.normal(ks[3], (C, H * L), jnp.float32) * s, 'Wq_up_c': jax.random.normal(ks[4], (L, DHE), jnp.float32) * s, 'Wq_up_e': jax.random.normal(ks[5], (L, DHE), jnp.float32) * s, 'Wk_up_c': jax.random.normal(ks[6], (L, DHE), jnp.float32) * s, 'Wk_up_e': jax.random.normal(ks[7], (L, DHE), jnp.float32) * s, 'Wv_up': jax.random.normal(ks[8], (L, DH), jnp.float32) * s, 'Wc': jax.random.normal(ks[9], (C, C), jnp.float32) * s}
    _L0_attn_in = _L0_attn_setup()

    def _L0_ffn_setup():
        import jax, jax.numpy as jnp
        import numpy as np
        B, S, D = (2, 512, 256)
        DFF = 512
        E_FFN = 8
        E_ZERO = 4
        E_TOT = E_FFN + E_ZERO
        TOP_K = 2
        key = jax.random.key(seed)
        k1, k2, k3, k4 = jax.random.split(key, 4)
        x = jax.random.normal(k1, (B, S, D), dtype=jnp.float32)
        gate_w = jax.random.normal(k2, (E_TOT, D), dtype=jnp.float32) * (1.0 / np.sqrt(D))
        expert_bias = jnp.zeros((E_TOT,), dtype=jnp.float32)
        w1 = jax.random.normal(k3, (E_FFN, DFF, D), dtype=jnp.float32) * (1.0 / np.sqrt(D))
        w2 = jax.random.normal(k4, (E_FFN, D, DFF), dtype=jnp.float32) * (1.0 / np.sqrt(DFF))
        return {'x': x, 'gate_w': gate_w, 'expert_bias': expert_bias, 'w1': w1, 'w2': w2}
    _L0_ffn_in = _L0_ffn_setup()
    _L0_c = _w((lambda *s: np.random.randn(*s).astype(np.float32) * 0.05)(4, 256))
    _L0_wmod = _w((lambda *s: np.random.randn(*s).astype(np.float32) * 0.05)(256, 6 * 256) * 256 ** (-0.5))
    _d = {'L0_attn_x': _L0_attn_in['x'], 'L0_attn_Wq_down': _L0_attn_in['Wq_down'], 'L0_attn_Wk_down': _L0_attn_in['Wk_down'], 'L0_attn_Wv_down': _L0_attn_in['Wv_down'], 'L0_attn_Wq_up_c': _L0_attn_in['Wq_up_c'], 'L0_attn_Wq_up_e': _L0_attn_in['Wq_up_e'], 'L0_attn_Wk_up_c': _L0_attn_in['Wk_up_c'], 'L0_attn_Wk_up_e': _L0_attn_in['Wk_up_e'], 'L0_attn_Wv_up': _L0_attn_in['Wv_up'], 'L0_attn_Wc': _L0_attn_in['Wc'], 'L0_ffn_gate_w': _L0_ffn_in['gate_w'], 'L0_ffn_expert_bias': _L0_ffn_in['expert_bias'], 'L0_ffn_w1': _L0_ffn_in['w1'], 'L0_ffn_w2': _L0_ffn_in['w2'], 'L0_c': _L0_c, 'L0_wmod': _L0_wmod}
    _x0 = _d['L0_attn_x']
    _d['L0_attn_x'] = jax.random.normal(jax.random.fold_in(jax.random.key(seed), 1), (4, 2048, 256), dtype=_x0.dtype)
    del _x0
    return _d

def reference(L0_attn_x, L0_attn_Wq_down, L0_attn_Wk_down, L0_attn_Wv_down, L0_attn_Wq_up_c, L0_attn_Wq_up_e, L0_attn_Wk_up_c, L0_attn_Wk_up_e, L0_attn_Wv_up, L0_attn_Wc, L0_ffn_gate_w, L0_ffn_expert_bias, L0_ffn_w1, L0_ffn_w2, L0_c, L0_wmod):

    def _L0_attn_ref(x, Wq_down, Wk_down, Wv_down, Wq_up_c, Wq_up_e, Wk_up_c, Wk_up_e, Wv_up, Wc):
        import jax, jax.numpy as jnp
        import numpy as np
        import math
        B, T, C = (2, 512, 256)
        H, L = (16, 64)
        DH = C // H
        DHE = DH // 2
        THETA = 10000.0

        def _rope_cache(t, dim):
            inv_freq = 1.0 / THETA ** (jnp.arange(0, dim, 2, dtype=jnp.float32) / dim)
            freqs = jnp.arange(t, dtype=jnp.float32)[:, None] * inv_freq[None, :]
            emb = jnp.concatenate((freqs, freqs), axis=-1)
            return (jnp.cos(emb), jnp.sin(emb))

        def _apply_rope(x, cos, sin):
            x1 = x[..., 0::2]
            x2 = x[..., 1::2]
            rot = jnp.stack((-x2, x1), axis=-1).reshape(x.shape)
            return x * cos[None, None] + rot * sin[None, None]
        b, t, c = x.shape
        q_lat = (x @ Wq_down).reshape(b, t, H, L)
        k_lat = (x @ Wk_down).reshape(b, t, H, L)
        v_lat = (x @ Wv_down).reshape(b, t, H, L)
        q_c = jnp.einsum('bthl,ld->bhtd', q_lat, Wq_up_c)
        q_e = jnp.einsum('bthl,ld->bhtd', q_lat, Wq_up_e)
        k_c = jnp.einsum('bthl,ld->bhtd', k_lat, Wk_up_c)
        k_e = jnp.einsum('bthl,ld->bhtd', k_lat, Wk_up_e)
        v = jnp.einsum('bthl,ld->bhtd', v_lat, Wv_up)
        cos, sin = _rope_cache(t, DHE)
        q = jnp.concatenate([q_c, _apply_rope(q_e, cos, sin)], axis=-1)
        k = jnp.concatenate([k_c, _apply_rope(k_e, cos, sin)], axis=-1)
        scale = 1.0 / math.sqrt(DH)
        scores = jnp.einsum('bhqd,bhkd->bhqk', q, k) * scale
        causal = jnp.tril(jnp.ones((t, t), dtype=bool))
        scores = jnp.where(causal[None, None], scores, -jnp.inf)
        att = jax.nn.softmax(scores, axis=-1)
        y = jnp.einsum('bhqk,bhkd->bhqd', att, v)
        y = y.transpose(0, 2, 1, 3).reshape(b, t, c)
        return y @ Wc

    def _L0_ffn_ref(x, gate_w, expert_bias, w1, w2):
        import jax, jax.numpy as jnp
        import numpy as np
        B, S, D = (2, 512, 256)
        DFF = 512
        E_FFN = 8
        E_ZERO = 4
        E_TOT = E_FFN + E_ZERO
        TOP_K = 2
        logits = jnp.einsum('btd,ed->bte', x, gate_w) + expert_bias
        topk_logits, topk_idx = jax.lax.top_k(logits, TOP_K)
        topk_w = jax.nn.softmax(topk_logits, axis=-1)
        onehot = jax.nn.one_hot(topk_idx, E_TOT, dtype=x.dtype)
        w = jnp.einsum('btk,btke->bte', topk_w, onehot)
        w_ffn = w[..., :E_FFN]
        w_zero = jnp.sum(w[..., E_FFN:], axis=-1)
        h = jax.nn.silu(jnp.einsum('btd,efd->btef', x, w1))
        y = jnp.einsum('btef,edf->bted', h, w2)
        out = jnp.einsum('bte,bted->btd', w_ffn, y) + w_zero[..., None] * x
        return out
    x = L0_attn_x
    mod = (_silu(L0_c) @ L0_wmod).reshape(L0_c.shape[0], 6, 1, -1)
    sa, ca, ga, sb, cb, gb = (mod[:, 0], mod[:, 1], mod[:, 2], mod[:, 3], mod[:, 4], mod[:, 5])
    ga = (2 * (ga >= 0) - 1) * jnp.maximum(jnp.abs(ga), 0.25)
    gb = (2 * (gb >= 0) - 1) * jnp.maximum(jnp.abs(gb), 0.25)
    h = _layernorm(x, axis=-1) * (1 + ca) + sa
    x = x + ga * _L0_attn_ref(h, L0_attn_Wq_down, L0_attn_Wk_down, L0_attn_Wv_down, L0_attn_Wq_up_c, L0_attn_Wq_up_e, L0_attn_Wk_up_c, L0_attn_Wk_up_e, L0_attn_Wv_up, L0_attn_Wc)
    h = _layernorm(x, axis=-1) * (1 + cb) + sb
    x = x + gb * _L0_ffn_ref(h, L0_ffn_gate_w, L0_ffn_expert_bias, L0_ffn_w1, L0_ffn_w2)
    return x

_drawn_inputs = setup_inputs


def setup_inputs(seed=0):
    import zlib

    import numpy as np

    out = dict(_drawn_inputs(seed))
    spreads = {'L0_ffn_expert_bias': (0.0, 0.361)}
    factors = {'L0_attn_Wq_down': 8.0,
     'L0_attn_Wk_down': 8.0,
     'L0_attn_Wv_down': 8.0,
     'L0_attn_Wq_up_c': 8.0,
     'L0_attn_Wq_up_e': 8.0,
     'L0_attn_Wk_up_c': 8.0,
     'L0_attn_Wk_up_e': 8.0,
     'L0_attn_Wv_up': 8.0,
     'L0_attn_Wc': 8.0}
    for name, (base, spread) in spreads.items():
        noise = np.random.default_rng([zlib.crc32(name.encode()), seed]).standard_normal(out[name].shape)
        drawn = base * np.exp(spread * noise) if base else spread * noise
        out[name] = jnp.asarray(drawn.astype(out[name].dtype))
    for name, factor in factors.items():
        out[name] = (out[name] * factor).astype(out[name].dtype)
    return out
```

```python
from contextlib import ExitStack

import numpy as np

import concourse.bass as bass
from concourse import mybir

ALU = mybir.AluOpType
ACT = mybir.ActivationFunctionType
F32 = mybir.dt.float32
BF16 = mybir.dt.bfloat16
I32 = mybir.dt.int32
U32 = mybir.dt.uint32
AX_X = mybir.AxisListType.X

P = 128
B, T, C = 4, 2048, 256
H, L, DH = 16, 64, 16
KC = C // P
NTOK = B * T
NT = NTOK // P
TT = T // P
BLK = 512
NB = NTOK // BLK
TPB = BLK // P
BPS = T // BLK
EPS = 1e-5
HG = 4
NG = H // HG
NIT = B * NG
SLOT = 32
QB = 256
NJ = T // QB
COMBOS = [(0, 0), (0, 1), (1, 0), (1, 1), (0, 2), (2, 0)]
SROWS = 16 * len(COMBOS)
MROWS = 3
E, EZ, F = 8, 4, 512
ET = E + EZ
FC = F // P
NSLOT_T = 2 * NT + E
NSLOT = NSLOT_T * P
ZROW = NSLOT
BIG = 1e30


def apart(eng):
    eng.nop(nofuse=True)


class Steps:

    def __init__(self, eng, sem):
        self.eng, self.sem, self.base, self.n = eng, sem, 0, 0

    def at(self, base):
        self.base, self.n = base, 0

    def mark(self, ins):
        self.n += 1
        ins.then_inc(self.sem, 1)

    def wait(self):
        self.eng.wait_ge(self.sem, self.base + self.n)

    def link(self, ins):
        self.mark(ins)
        self.wait()


def wide(ap, dim, n):
    shape = list(ap.shape)
    shape[dim] = n
    return ap.broadcast_to(shape)


def blocks(eng, first, second):
    def sequence(b, last):
        for j in range(BPS):
            if j < BPS - 1:
                first(b, j + 1)
            elif not last:
                first(b + 1, 0)
            second(b, j)

    first(0, 0)
    with eng.Fori(0, B - 1) as b:
        sequence(b, False)
    sequence(B - 1, True)


def build(nc, a, out):
    d = {}
    with ExitStack() as ctx:
        def dram(name, shape, dt):
            d[name] = nc.dram_tensor(name, shape, dt, kind="Internal").ap()

        dram("q_parts", (3, B, H, DH, T), BF16)
        dram("k_parts", (3, B, H, DH, T), BF16)
        dram("v_ones", (B, NG, P, TT, HG * SLOT), F32)
        dram("attn_t", (B, NG, P, T), F32)
        dram("x_mid", (NTOK, C), F32)
        dram("slot_x", (NSLOT + 2 * NTOK, C), F32)
        dram("slot_y", (NSLOT + P, C), F32)

        def sb(name, shape, dt=F32):
            return ctx.enter_context(nc.sbuf_tensor(name, shape, dt))

        ps = ctx.enter_context(nc.psum_tensor("ps", [P, 8, 512], F32))
        k = {
            "ident": sb("ident", [P, P]),
            "identb": sb("identb", [P, P], BF16),
            "mask_qk": sb("mask_qk", [P, P], BF16),
            "mask_kq": sb("mask_kq", [P, P], BF16),
            "mod": sb("mod", [P, 12, B]),
            "ca1": sb("ca1", [P, KC, B]),
            "sbc": sb("sbc", [P, B, 2, C]),
            "gb": sb("gb", [P, B, C]),
            "wc": sb("wc", [P, B, KC, C]),
            "gate": sb("gate", [P, KC, ET]),
            "bias": sb("bias", [P, ET]),
            "eps": sb("eps", [P, 1]),
        }
        with ExitStack() as c2:
            wf = c2.enter_context(nc.sbuf_tensor("w_fused", [P, 3, KC, C], F32))
            setup(nc, a, k, wf, ps)
            project(nc, a, d, k, wf, ps)
        attention(nc, d, k, ps)
        with ExitStack() as c2:
            r = {n: c2.enter_context(nc.sbuf_tensor(n, s, F32)) for n, s in {
                "h2": [P, NT, C], "w12": [P, NT, 2], "wz": [P, NT], "top2": [P, NT, 2]}.items()}
            r["idx2"] = c2.enter_context(nc.sbuf_tensor("idx2", [P, NT, 2], U32))
            r["pos"] = [c2.enter_context(nc.sbuf_tensor(f"pos{s}", [P, NT], I32)) for s in range(2)]
            r["gpos"] = [c2.enter_context(nc.sbuf_tensor(f"gpos{s}", [P, NT], I32)) for s in range(2)]
            route(nc, a, d, k, r, ps)
            with ExitStack() as c3:
                w = {n: c3.enter_context(nc.sbuf_tensor(n, s, F32)) for n, s in {
                    "w1t": [P, E, KC, F], "w2t": [P, E, FC, C]}.items()}
                w["eid"] = c3.enter_context(nc.sbuf_tensor("eid", [P, NSLOT_T], I32))
                place(nc, a, d, k, r, w, ps)
                experts(nc, d, k, w, ps)
            combine(nc, d, k, r, out)


def setup(nc, a, k, wf, ps):
    with ExitStack() as ctx:
        def sb(name, shape, dt=F32):
            return ctx.enter_context(nc.sbuf_tensor(name, shape, dt))

        def sem(name):
            return ctx.enter_context(nc.semaphore(name))

        c_in, c_sig = sb("c_in", [B, C]), sb("c_sig", [B, C])
        gate_in = sb("gate_in", [ET, C])
        down = sb("down", [P, 3, KC, H * L])
        down_t = sb("down_t", [P, 3, H // 2, C])
        up = sb("up", [P, 3, 32])
        wmod = sb("wmod", [P, KC, 6 * C])
        wc_in = sb("wc_in", [P, KC, C])
        c_t = sb("c_t", [P, KC, B])
        masks = sb("masks", [P, 2, P])
        c_rep = sb("c_rep", [P, KC, B, P])
        g_rows = sb("g_rows", [P, B, 2, C])
        g_sign = sb("g_sign", [P, B, 2, C])
        ld_small, ld_down, ld_mod, up_zero, ld_up = (sem(f"s_{n}") for n in ("small", "down", "mod", "upz", "up"))
        sig_done, pe_unit, evac, dve_step = (sem(f"s_{n}") for n in ("sig", "pe", "evac", "dve"))
        downs = ["L0_attn_Wq_down", "L0_attn_Wk_down", "L0_attn_Wv_down"]
        ups = [["L0_attn_Wq_up_c", "L0_attn_Wq_up_e"], ["L0_attn_Wk_up_c", "L0_attn_Wk_up_e"], ["L0_attn_Wv_up"]]
        NSMALL = 7
        NU_DOWN = 2
        NU_MOD = NU_DOWN + 12
        NU_ROWS = NU_MOD + 1
        NU_FUSE = NU_ROWS + 2 * B
        with nc.Block() as block:
            @block.sync
            def _(sp):
                sp.dma_start(c_in[:, :], a["L0_c"]).then_inc(ld_small, 16)
                sp.dma_start(gate_in[:, :], a["L0_ffn_gate_w"]).then_inc(ld_small, 16)
                sp.dma_start(k["ident"][:, :], a["ident"]).then_inc(ld_small, 16)
                sp.dma_start(masks[:, 0, :], a["mask_qk"]).then_inc(ld_small, 16)
                sp.dma_start(masks[:, 1, :], a["mask_kq"]).then_inc(ld_small, 16)
                bias = a["L0_ffn_expert_bias"].rearrange("(o e) -> o e", o=1)
                sp.dma_start(k["bias"][:, :], bias.broadcast_to([P, ET])).then_inc(ld_small, 16)
                sp.dma_start(wc_in[:, :, :], a["L0_attn_Wc"].rearrange("(c p) n -> p c n", p=P)).then_inc(ld_small, 16)
                for x in range(3):
                    sp.dma_start(down[:, x, :, :], a[downs[x]].rearrange("(c p) n -> p c n", p=P)).then_inc(ld_down, 16)
                sp.dma_start(wmod[:, :, :], a["L0_wmod"].rearrange("(c p) n -> p c n", p=P)).then_inc(ld_mod, 16)
                sp.wait_ge(up_zero, 1)
                for x in range(3):
                    for half in range(2):
                        for n, name in enumerate(ups[x]):
                            w = DH // len(ups[x])
                            sp.dma_start(up[half * L:(half + 1) * L, x, half * DH + n * w:half * DH + (n + 1) * w],
                                         a[name]).then_inc(ld_up, 16)

            @block.scalar
            def _(act):
                act.wait_ge(ld_small, 16 * NSMALL)
                act.activation(c_sig[:, :], c_in[:, :], ACT.Sigmoid).then_inc(sig_done, 1)

            @block.tensor
            def _(pe):
                unit = [0]

                def begin():
                    if unit[0] >= 8:
                        pe.wait_ge(evac, unit[0] - 7)
                    return ps[:, unit[0] % 8, :]

                def end(ins):
                    unit[0] += 1
                    ins.then_inc(pe_unit, 1)

                pe.wait_ge(dve_step, 1)
                o = begin()
                for c in range(KC):
                    ins = pe.transpose(o[:, B * c:B * c + B], c_in[:, c * P:(c + 1) * P], k["ident"][0:B, 0:B])
                end(ins)
                o = begin()
                for c in range(KC):
                    ins = pe.transpose(o[:, ET * c:ET * c + ET], gate_in[:, c * P:(c + 1) * P], k["ident"][0:ET, 0:ET])
                end(ins)
                pe.wait_ge(ld_down, 48)
                for x in range(3):
                    for pp in range(H // 4):
                        o = begin()
                        for q in range(2):
                            for c in range(KC):
                                pair = 2 * pp + q
                                ins = pe.transpose(o[:, (q * KC + c) * P:(q * KC + c + 1) * P],
                                                   down[:, x, c, pair * P:(pair + 1) * P], k["ident"][:, :])
                        end(ins)
                pe.wait_ge(ld_mod, 16)
                pe.wait_ge(evac, 1)
                o = begin()
                for j in range(12):
                    for c in range(KC):
                        ins = pe.matmul(o[:, j * B:(j + 1) * B], wmod[:, c, j * P:(j + 1) * P], c_t[:, c, :],
                                        start=(c == 0), stop=(c == KC - 1))
                end(ins)
                pe.wait_ge(dve_step, 2)
                for first, second in ((2, 5), (3, 4)):
                    for b in range(B):
                        o = begin()
                        for n, g in enumerate((first, second)):
                            for c in range(KC):
                                ins = pe.matmul(o[:, n * C:(n + 1) * C], c_rep[:, c, b, :], wmod[:, c, g * C:(g + 1) * C],
                                                start=(c == 0), stop=(c == KC - 1))
                        end(ins)
                pe.wait_ge(ld_up, 16 * 10)
                pe.wait_ge(evac, NU_MOD)
                for x in range(3):
                    o = begin()
                    for c in range(KC):
                        for pair in range(H // 2):
                            at = c * C + 32 * pair
                            ins = pe.matmul(o[:, at:at + 32], down_t[:, x, pair, c * P:(c + 1) * P], up[:, x, :],
                                            start=True, stop=True)
                    end(ins)

            @block.vector
            def _(dve):
                unit = [0]

                def begin():
                    dve.wait_ge(pe_unit, unit[0] + 1)
                    o = ps[:, unit[0] % 8, :]
                    unit[0] += 1
                    return o

                dve.memset(up[:, :, :], 0.0).then_inc(up_zero, 1)
                dve.memset(k["eps"][:, :], EPS)
                dve.wait_ge(sig_done, 1)
                dve.tensor_tensor(c_in[:, :], c_in[:, :], c_sig[:, :], ALU.mult).then_inc(dve_step, 1)
                dve.tensor_copy(c_t[:, :, :], begin()[:, 0:KC * B]).then_inc(evac, 1)
                dve.wait_ge(evac, 1)
                dve.tensor_copy(c_rep[:, :, :, :], wide(c_t[:, :, :, None], 3, P)).then_inc(dve_step, 1)
                dve.tensor_copy(k["gate"][:, :, :], begin()[:, 0:KC * ET]).then_inc(evac, 1)
                for x in range(3):
                    for pp in range(H // 4):
                        dve.tensor_copy(down_t[:, x, 2 * pp:2 * pp + 2, :], begin()[:, :]).then_inc(evac, 1)
                dve.tensor_copy(k["mod"][:, :, :], begin()[:, 0:12 * B]).then_inc(evac, 1)
                for b in range(B):
                    dve.tensor_copy(g_rows[:, b, :, :], begin()[:, :]).then_inc(evac, 1)
                for b in range(B):
                    o = begin()
                    dve.tensor_copy(k["sbc"][:, b, 0, :], o[:, 0:C])
                    dve.tensor_scalar(k["sbc"][:, b, 1, :], o[:, C:2 * C], 1.0, None, ALU.add).then_inc(evac, 1)
                for x in range(3):
                    dve.tensor_copy(wf[:, x, :, :], begin()[:, :]).then_inc(evac, 1)
                dve.wait_ge(evac, NU_FUSE)
                dve.tensor_copy(k["identb"][:, :], k["ident"][:, :])
                dve.tensor_copy(k["mask_qk"][:, :], masks[:, 0, :])
                dve.tensor_copy(k["mask_kq"][:, :], masks[:, 1, :])
                dve.tensor_scalar(k["ca1"][:, :, :], k["mod"][:, 2:4, :], 1.0, None, ALU.add).then_inc(dve_step, 1)
                dve.tensor_scalar(g_sign[:, :, :, :], g_rows[:, :, :, :], 0.0, 2.0, ALU.is_ge, ALU.mult).then_inc(dve_step, 1)
                dve.wait_ge(dve_step, 4)
                dve.tensor_scalar(g_sign[:, :, :, :], g_sign[:, :, :, :], -1.0, None, ALU.add).then_inc(dve_step, 1)
                dve.wait_ge(dve_step, 5)
                dve.tensor_tensor(g_rows[:, :, :, :], g_rows[:, :, :, :], g_sign[:, :, :, :], ALU.mult).then_inc(dve_step, 1)
                dve.wait_ge(dve_step, 6)
                dve.tensor_scalar(g_rows[:, :, :, :], g_rows[:, :, :, :], 0.25, None, ALU.max).then_inc(dve_step, 1)
                dve.wait_ge(dve_step, 7)
                dve.tensor_tensor(g_rows[:, :, :, :], g_rows[:, :, :, :], g_sign[:, :, :, :], ALU.mult).then_inc(dve_step, 1)
                dve.wait_ge(dve_step, 8)
                dve.tensor_copy(k["gb"][:, :, :], g_rows[:, :, 1, :]).then_inc(dve_step, 1)
                for b in range(B):
                    for c in range(KC):
                        dve.tensor_tensor(k["wc"][:, b, c, :], wc_in[:, c, :], g_rows[:, b, 0, :],
                                          ALU.mult).then_inc(dve_step, 1)


def project(nc, a, d, k, wf, ps):
    with ExitStack() as ctx:
        def sb(name, shape, dt=F32):
            return ctx.enter_context(nc.sbuf_tensor(name, shape, dt))

        def sem(name):
            return ctx.enter_context(nc.semaphore("p_" + name))

        NU = 4
        cos, sin = sb("cos", [P, T]), sb("sin", [P, T])
        xin = sb("xin", [P, BPS, TPB, C])
        stats, mv = sb("stats", [P, TPB, 6]), sb("mv", [P, TPB, 2])
        std, rstd = sb("std", [P, TPB]), sb("rstd", [P, TPB])
        h_t = sb("h_t", [P, KC, BLK])
        raw, rot = sb("raw", [P, NU, BLK]), sb("rot", [P, NU, BLK])
        parts = sb("parts", [P, 2, 3, NU, BLK], BF16)
        vout = sb("vout", [P, 2, TPB, H, SLOT])
        tab_ld, norm_step, std_done, hn_done, tr_done, ht_done, ones_done = (
            sem(n) for n in ("tab", "norm", "std", "hn", "tr", "ht", "ones"))
        qk_done, v_done, copy_done, vcopy_done, rope_step, cos_done, hi_done, mid_done, low_done = (
            sem(n) for n in ("qk", "v", "copy", "vcopy", "rope", "cos", "hi", "mid", "low"))
        x_ld = [sem(f"x{j}") for j in range(BPS)]
        st_parts = [sem(f"stp{j}") for j in range(2)]
        st_v = [sem(f"stv{j}") for j in range(2)]
        x_v = a["L0_attn_x"].rearrange("b (n j p) c -> b n p j c", p=P, j=TPB)
        NPART = 3 * NU * 16
        NV = TPB * 16
        NORM, ROPE = 3, 4
        hp, qk, vp = ps[:, 0:2, :], ps[:, 2:6, :], ps[:, 6:8, :]

        with nc.Block() as block:
            @block.sync
            def _(sp):
                for s in (low_done, ht_done, v_done, copy_done, vcopy_done, *st_parts, *st_v):
                    sp.sem_inc(s, 1)
                sp.dma_start(cos[:, :], a["cos"]).then_inc(tab_ld, 16)
                sp.dma_start(sin[:, :], a["sin"]).then_inc(tab_ld, 16)

                def load(b, j):
                    sp.dma_start(xin[:, j, :, :], x_v[bass.ds(b, 1), j].rearrange("o p j c -> (o p) j c")).then_inc(x_ld[j], 16)

                def store(b, j):
                    par, tok = j % 2, j * BLK
                    sp.wait_ge(vcopy_done, BPS * b + j + 2)
                    for n in range(TPB):
                        dst = d["v_ones"][bass.ds(b, 1), :, :, TPB * j + n, :]
                        sp.dma_start(dst.rearrange("o g p n -> (o p) g n"),
                                     vout[:, par, n, :, :].rearrange("p (g h) s -> p g (h s)", g=NG)).then_inc(st_v[par], 16)
                    sp.wait_ge(low_done, BPS * b + j + 2)
                    for x, name in enumerate(("q_parts", "k_parts")):
                        for m in range(2):
                            for part in range(3):
                                dst = d[name][part, bass.ds(b, 1), 8 * m:8 * m + 8, :, tok:tok + BLK]
                                sp.dma_start(dst.rearrange("o h d t -> (o h d) t"),
                                             parts[:, par, part, 2 * x + m, :]).then_inc(st_parts[par], 16)

                def sequence(b, last):
                    for j in range(BPS):
                        if not last:
                            sp.wait_ge(tr_done, BPS * b + j + 1)
                            load(b + 1, j)
                        store(b, j)

                for j in range(BPS):
                    load(0, j)
                with sp.Fori(0, B - 1) as b:
                    sequence(b, False)
                sequence(B - 1, True)
                for par in range(2):
                    sp.wait_ge(st_parts[par], NPART * NB // 2 + 1)
                    sp.wait_ge(st_v[par], NV * NB // 2 + 1)

            @block.vector
            def _(dve):
                dve.memset(vout[:, :, :, :, :], 1.0).then_inc(ones_done, 1)
                dve.wait_ge(tab_ld, 32)

                def norm(b, j):
                    t = BPS * b + j
                    dve.wait_ge(x_ld[j], 16 * b + 16)
                    for n in range(TPB):
                        ins = dve.bn_stats(stats[:, n, :], xin[:, j, n, :])
                    ins.then_inc(norm_step, 1)
                    dve.wait_ge(norm_step, NORM * t + 1)
                    apart(dve)
                    for n in range(TPB):
                        ins = dve.bn_aggr(mv[:, n, :], stats[:, n, :])
                    ins.then_inc(norm_step, 1)
                    dve.wait_ge(std_done, t + 1)
                    dve.reciprocal(rstd[:, :], std[:, :]).then_inc(norm_step, 1)
                    dve.wait_ge(norm_step, NORM * t + 3)
                    for n in range(TPB):
                        ins = dve.tensor_scalar(xin[:, j, n, :], xin[:, j, n, :], mv[:, n, 0:1],
                                                rstd[:, n:n + 1], ALU.subtract, ALU.mult)
                    ins.then_inc(hn_done, 1)

                def rope(b, j):
                    t, tok = BPS * b + j, j * BLK
                    dve.wait_ge(copy_done, t + 2)
                    apart(dve)
                    dve.stream_shuffle(rot[:, :, :], raw[:, :, :], [r ^ 1 for r in range(32)]).then_inc(rope_step, 1)
                    dve.wait_ge(rope_step, ROPE * t + 1)
                    dve.tensor_tensor(rot[:, :, :], rot[:, :, :], wide(sin[:, None, tok:tok + BLK], 1, NU),
                                      ALU.mult).then_inc(rope_step, 1)
                    dve.wait_ge(rope_step, ROPE * t + 2)
                    dve.wait_ge(cos_done, t + 1)
                    dve.tensor_tensor(raw[:, :, :], raw[:, :, :], rot[:, :, :], ALU.add).then_inc(rope_step, 1)
                    dve.wait_ge(hi_done, t + 1)
                    dve.tensor_tensor(raw[:, :, :], raw[:, :, :], parts[:, j % 2, 0, :, :],
                                      ALU.subtract).then_inc(rope_step, 1)

                blocks(dve, norm, rope)

            @block.gpsimd
            def _(pool):
                pool.wait_ge(tab_ld, 32)

                def nothing(b, j):
                    pass

                def low(b, j):
                    t, tok = BPS * b + j, j * BLK
                    pool.wait_ge(rope_step, ROPE * t + 1)
                    pool.tensor_tensor(raw[:, :, :], raw[:, :, :], wide(cos[:, None, tok:tok + BLK], 1, NU),
                                       ALU.mult).then_inc(cos_done, 1)
                    pool.wait_ge(mid_done, t + 1)
                    pool.tensor_tensor(parts[:, j % 2, 2, :, :], raw[:, :, :], parts[:, j % 2, 1, :, :],
                                       ALU.subtract).then_inc(low_done, 1)

                blocks(pool, nothing, low)

            @block.scalar
            def _(act):
                act.wait_ge(ones_done, 1)

                def norm(b, j):
                    t = BPS * b + j
                    act.wait_ge(norm_step, NORM * t + 2)
                    act.activation(std[:, :], mv[:, :, 1], ACT.Sqrt, bias=k["eps"][:, :]).then_inc(std_done, 1)
                    act.wait_ge(tr_done, t + 1)
                    act.wait_ge(v_done, t + 1)
                    apart(act)
                    for c in range(KC):
                        ins = act.activation(h_t[:, c, :], hp[:, c, :], ACT.Identity, bias=k["mod"][:, c, bass.ds(b, 1)],
                                             scale=k["ca1"][:, c, bass.ds(b, 1)])
                    ins.then_inc(ht_done, 1)

                def split(b, j):
                    t, par, n = BPS * b + j, j % 2, 2 * b + j // 2
                    act.wait_ge(qk_done, t + 1)
                    act.wait_ge(low_done, t + 1)
                    act.copy(raw[:, :, :], qk).then_inc(copy_done, 1)
                    act.wait_ge(v_done, t + 2)
                    act.wait_ge(st_v[par], NV * n + 1)
                    act.copy(vout[:, par, :, :, 0:DH], vp.rearrange("p n (j h s) -> p (n j) h s", h=H, s=DH)).then_inc(vcopy_done, 1)
                    act.wait_ge(rope_step, ROPE * t + 3)
                    act.wait_ge(st_parts[par], NPART * n + 1)
                    act.copy(parts[:, par, 0, :, :], raw[:, :, :]).then_inc(hi_done, 1)
                    act.wait_ge(rope_step, ROPE * t + 4)
                    act.copy(parts[:, par, 1, :, :], raw[:, :, :]).then_inc(mid_done, 1)

                blocks(act, norm, split)

            @block.tensor
            def _(pe):
                def transposes(b, j):
                    t = BPS * b + j
                    pe.wait_ge(hn_done, t + 1)
                    pe.wait_ge(ht_done, t + 1)
                    for n in range(TPB):
                        for c in range(KC):
                            ins = pe.transpose(hp[:, c, n * P:(n + 1) * P], xin[:, j, n, c * P:(c + 1) * P], k["ident"][:, :])
                    ins.then_inc(tr_done, 1)

                def products(b, j):
                    t = BPS * b + j
                    pe.wait_ge(ht_done, t + 2)
                    pe.wait_ge(copy_done, t + 1)
                    for x in range(2):
                        for m in range(2):
                            for c in range(KC):
                                ins = pe.matmul(qk[:, 2 * x + m, :], wf[:, x, c, m * P:(m + 1) * P], h_t[:, c, :],
                                                start=(c == 0), stop=(c == KC - 1))
                    ins.then_inc(qk_done, 1)
                    pe.wait_ge(vcopy_done, t + 1)
                    for n in range(TPB):
                        for c in range(KC):
                            ins = pe.matmul(vp[:, n // 2, (n % 2) * C:(n % 2 + 1) * C], h_t[:, c, n * P:(n + 1) * P],
                                            wf[:, 2, c, :], start=(c == 0), stop=(c == KC - 1))
                    ins.then_inc(v_done, 1)

                blocks(pe, transposes, products)


def attention(nc, d, k, ps):
    with ExitStack() as ctx:
        def sb(name, shape, dt=F32):
            return ctx.enter_context(nc.sbuf_tensor(name, shape, dt))

        def sem(name):
            return ctx.enter_context(nc.semaphore("a_" + name))

        R = 3
        NP = 3
        STEPS = [(J, j) for J in range(NJ) for j in range(QB // P * (J + 1))]
        NS = len(STEPS)
        LAST = {J: max(s for s, (JJ, _) in enumerate(STEPS) if JJ == J) for J in range(NJ)}
        UNITS = [(i, g, c) for i in range(TT) for g in range(HG) for c in range(i // 4 + 1)]
        NUNIT = len(UNITS) + 2
        SPREAD = NS - 10
        at_step = [[u for u in range(len(UNITS)) if u * SPREAD // len(UNITS) == s] for s in range(NS)]
        MAX_STEP = SPREAD + 1
        NMAX = 9
        ks, qs = sb("ks", [P, R, HG, T], BF16), sb("qs", [P, R, HG, T], BF16)
        vs = sb("vs", [P, R, TT, HG * SLOT])
        probs = sb("probs", [P, NP, HG, QB])
        o_sb = sb("o_sb", [P, 2, QB])
        mxc, negm, res = sb("mxc", [P, HG, TT, 4]), sb("negm", [P, HG, TT]), sb("res", [P, HG, TT])
        mparts = sb("mparts", [P, MROWS, HG * TT], BF16)
        m_t = sb("m_t", [HG * TT, MROWS, P], BF16)
        zero = sb("zero", [P, 8 * C])
        ld = [sem(f"ld{r}") for r in range(R)]
        m_ld, init_done, red_ready, red_done, max_step, mt_done = (
            sem(n) for n in ("mld", "init", "redr", "redd", "max", "mt"))
        st_ready, exp_done, pv_done, o_done, zero_set, zero_st = (sem(n) for n in ("str", "exp", "pv", "o", "zset", "zst"))
        o_st = [sem(f"ost{r}") for r in range(2)]
        LD = 16 * (2 * len(COMBOS) + 1)
        M_LD = 16 * MROWS
        st_ps = ps[:, 0:4, :].rearrange("p (u n) (g q) -> p u (n g) q", u=2, g=2)
        red_ps, o_ps = ps[:, 4:6, :], ps[:, 6:8, :]
        assert NS % 2 == 0 and NS % NP == 0 and NUNIT % 2 == 0 and NIT % R == 1

        def iterations(eng, step):
            step((0, 0), None)
            with eng.Fori(0, NIT // R) as i:
                for r in range(R):
                    n = R * i + r
                    step((n + 1, (r + 1) % R), (n, r))
            step(None, (NIT - 1, (NIT - 1) % R))

        with nc.Block() as block:
            @block.sync
            def _(sp):
                sp.sem_inc(red_done, 2)
                sp.sem_inc(exp_done, 2)
                sp.sem_inc(pv_done, NP)
                sp.sem_inc(o_done, 2)
                sp.sem_inc(m_ld, 1)
                for r in range(2):
                    sp.sem_inc(o_st[r], 1)

                qv = d["q_parts"].rearrange("x b (g h) d t -> x (b g) d h t", h=HG)
                kv = d["k_parts"].rearrange("x b (g h) d t -> x (b g) d h t", h=HG)
                vv = d["v_ones"].rearrange("b g p j n -> (b g) p j n")
                ov = d["attn_t"].rearrange("b g p t -> (b g) p t")

                def load(n, r):
                    for m, (kp, qp) in enumerate(COMBOS):
                        sp.dma_start(ks[16 * m:16 * m + 16, r, :, :],
                                     kv[kp, bass.ds(n, 1)].rearrange("o d h t -> (o d) h t")).then_inc(ld[r], 16)
                        sp.dma_start(qs[16 * m:16 * m + 16, r, :, :],
                                     qv[qp, bass.ds(n, 1)].rearrange("o d h t -> (o d) h t")).then_inc(ld[r], 16)
                    sp.dma_start(vs[:, r, :, :], vv[bass.ds(n, 1)].rearrange("o p j n -> (o p) j n")).then_inc(ld[r], 16)

                def maxima(n, r):
                    sp.wait_ge(mt_done, n + 1)
                    for m in range(MROWS):
                        sp.dma_start(qs[SROWS + m:SROWS + m + 1, r, :, :].rearrange("o h (i t) -> o (h i) t", t=P),
                                     m_t[:, m, :]).then_inc(m_ld, 16)

                def step(a, b, more=True):
                    if b is None:
                        return maxima(*a)
                    n, r = b
                    for J in range(NJ):
                        if J == NJ - 1 and a is not None:
                            maxima(*a)
                        sp.wait_ge(o_done, NJ * n + J + 1 + 2)
                        sp.dma_start(ov[bass.ds(n, 1), :, J * QB:(J + 1) * QB].rearrange("o p t -> (o p) t"),
                                     o_sb[:, J % 2, :]).then_inc(o_st[J % 2], 16)
                    if more:
                        load(n + R, r)

                for n in range(R):
                    load(n, n)
                step((0, 0), None)
                full = (NIT - R) // R
                with sp.Fori(0, full) as i:
                    for r in range(R):
                        step((R * i + r + 1, (r + 1) % R), (R * i + r, r))
                for n in range(R * full, NIT):
                    step((n + 1, (n + 1) % R) if n + 1 < NIT else None, (n, n % R), n + R < NIT)
                for r in range(2):
                    sp.wait_ge(o_st[r], 16 * NIT * NJ // 2 + 1)

            @block.gpsimd
            def _(pool):
                pool.memset(zero[:, :], 0.0).then_inc(zero_set, 1)
                pool.wait_ge(zero_set, 1)
                rows = d["slot_x"][0:NSLOT, :].rearrange("(n p r) c -> n p (r c)", p=P, r=8)
                with pool.Fori(0, NSLOT // (8 * P)) as i:
                    pool.dma_start(rows[bass.ds(i, 1)].rearrange("o p n -> (o p) n"), zero[:, :]).then_inc(zero_st, 16)
                pool.dma_start(d["slot_y"][ZROW:ZROW + P, :], zero[:, 0:C]).then_inc(zero_st, 16)
                pool.wait_ge(zero_st, 16 * (NSLOT // (8 * P) + 1))

            @block.tensor
            def _(pe):
                def unit(n, r, u):
                    i, g, c = UNITS[u]
                    w = min(512, P * (i + 1) - 512 * c)
                    diag = c == i // 4
                    o = red_ps[:, u % 2, 0:w]
                    pe.wait_ge(red_done, NUNIT * n + u + 1)
                    ins = pe.matmul(o, qs[0:SROWS, r, g, i * P:(i + 1) * P], ks[0:SROWS, r, g, 512 * c:512 * c + w],
                                    start=True, stop=not diag)
                    if diag:
                        ins = pe.matmul(o[:, w - P:w], k["identb"][:, :], k["mask_qk"][:, :], start=False, stop=True)
                    ins.then_inc(red_ready, 1)

                def max_rows(n, r):
                    for h in range(2):
                        u = len(UNITS) + h
                        pe.wait_ge(max_step, NMAX * n + NMAX)
                        pe.wait_ge(red_done, NUNIT * n + u + 1)
                        apart(pe)
                        o = red_ps[0:HG * TT, u % 2, :].bitcast(BF16)
                        for m in range(2 if h == 0 else 1):
                            ins = pe.transpose(o[:, m * P:(m + 1) * P], mparts[:, 2 * h + m, :], k["identb"][:, :])
                        ins.then_inc(red_ready, 1)

                def scores(n, r, s):
                    J, j = STEPS[s]
                    lo = P if j == 2 * J + 1 else 0
                    pe.wait_ge(exp_done, NS * n + s + 1)
                    for g in range(HG):
                        o = st_ps[:, s % 2, g, 0:QB - lo]
                        diag = j >= 2 * J
                        ins = pe.matmul(o, ks[0:SROWS + MROWS, r, g, j * P:(j + 1) * P],
                                        qs[0:SROWS + MROWS, r, g, J * QB + lo:(J + 1) * QB], start=True, stop=not diag)
                        if diag:
                            ins = pe.matmul(o[:, 0:P], k["identb"][:, :], k["mask_kq"][:, :], start=False, stop=True)
                    ins.then_inc(st_ready, 1)

                def values(n, r, s):
                    J, j = STEPS[s]
                    lo = P if j == 2 * J + 1 else 0
                    if j == 0:
                        pe.wait_ge(o_done, NJ * n + J + 1)
                    pe.wait_ge(exp_done, NS * n + s + 1 + 2)
                    for g in range(HG):
                        ins = pe.matmul(o_ps[SLOT * g:SLOT * (g + 1), J % 2, lo:QB], vs[:, r, j, SLOT * g:SLOT * (g + 1)],
                                        probs[:, s % NP, g, 0:QB - lo], start=(j == 0), stop=(s == LAST[J]))
                    ins.then_inc(pv_done, 1)

                def loaded(n, r):
                    if isinstance(n, int):
                        pe.wait_ge(ld[r], LD * (n // R + 1))

                def step(a, b, count=None):
                    if a is not None:
                        pe.wait_ge(ld[a[1]], count)
                    if b is None:
                        for u in range(len(UNITS)):
                            unit(*a, u)
                        return max_rows(*a)
                    n, r = b
                    pe.wait_ge(m_ld, M_LD * n + M_LD + 1)
                    for s in range(NS):
                        scores(n, r, s)
                        if a is not None:
                            for u in at_step[s]:
                                unit(*a, u)
                            if s == MAX_STEP:
                                max_rows(*a)
                        if s > 0:
                            values(n, r, s - 1)
                    values(n, r, NS - 1)

                pe.wait_ge(init_done, 2)
                step((0, 0), None, LD)
                with pe.Fori(0, NIT // R) as i:
                    for r in range(R):
                        n = R * i + r
                        step((n + 1, (r + 1) % R), (n, r), LD * i + LD * ((r + 1) // R + 1))
                step(None, (NIT - 1, (NIT - 1) % R))

            @block.scalar
            def _(act):
                def step(a, b):
                    if b is None:
                        return
                    n, r = b
                    for s in range(NS):
                        J, j = STEPS[s]
                        w = P if j == 2 * J + 1 else QB
                        act.wait_ge(st_ready, NS * n + s + 1)
                        act.wait_ge(pv_done, NS * n + s + 1)
                        act.activation(probs[:, s % NP, :, 0:w], st_ps[:, s % 2, :, 0:w], ACT.Exp,
                                       scale=DH ** -0.5).then_inc(exp_done, 1)

                iterations(act, step)

            @block.vector
            def _(dve):
                dve.memset(mxc[:, :, :, :], -3e38)
                for r in range(R):
                    ins = dve.memset(ks[SROWS:SROWS + MROWS, r, :, :], 1.0)
                ins.then_inc(init_done, 2)
                dve.wait_ge(init_done, 2)

                def unit(n, u):
                    i, g, c = UNITS[u]
                    w = min(512, P * (i + 1) - 512 * c)
                    dve.wait_ge(red_ready, NUNIT * n + u + 1)
                    dve.tensor_reduce(mxc[:, g, i, c:c + 1], red_ps[:, u % 2, 0:w], AX_X, ALU.max).then_inc(red_done, 1)

                def maxima(n):
                    at = NMAX * n

                    def link(q, ins):
                        ins.then_inc(max_step, 1)
                        dve.wait_ge(max_step, at + q)

                    mp = mparts[:, :, :].rearrange("p m (g i) -> p m g i", g=HG)
                    dve.wait_ge(red_done, NUNIT * n + len(UNITS) + 2)
                    link(1, dve.tensor_reduce(negm[:, :, :], mxc[:, :, :, :], AX_X, ALU.max))
                    link(2, dve.tensor_scalar(negm[:, :, :], negm[:, :, :], -1.0, None, ALU.mult))
                    link(3, dve.tensor_copy(mp[:, 0], negm[:, :, :]))
                    link(4, dve.tensor_tensor(res[:, :, :], negm[:, :, :], mp[:, 0], ALU.subtract))
                    link(5, dve.tensor_copy(mp[:, 1], res[:, :, :]))
                    link(6, dve.tensor_tensor(res[:, :, :], res[:, :, :], mp[:, 1], ALU.subtract))
                    link(7, dve.tensor_copy(mp[:, 2], res[:, :, :]))
                    dve.nop().then_inc(max_step, 2)

                def max_rows(n):
                    dve.wait_ge(m_ld, M_LD * n + 1)
                    for h in range(2):
                        u = len(UNITS) + h
                        w = 2 - h
                        dve.wait_ge(red_ready, NUNIT * n + u + 1)
                        ins = dve.tensor_copy(m_t[:, 2 * h:2 * h + w, :],
                                              red_ps[0:HG * TT, u % 2, :].bitcast(BF16)[:, 0:w * P])
                        ins.then_inc(red_done, 1)
                    dve.wait_ge(red_done, NUNIT * n + NUNIT + 2)
                    dve.nop().then_inc(mt_done, 1)

                def output(n, J):
                    dve.wait_ge(pv_done, NS * n + LAST[J] + 1 + NP)
                    dve.wait_ge(o_st[J % 2], 16 * (NJ // 2 * n + J // 2) + 1)
                    dve.tensor_copy(o_sb[:, J % 2, :], o_ps[:, J % 2, 0:QB]).then_inc(o_done, 1)

                def step(a, b):
                    if b is None:
                        for u in range(len(UNITS)):
                            unit(a[0], u)
                        maxima(a[0])
                        return max_rows(a[0])
                    n, r = b
                    for s in range(NS):
                        if a is not None:
                            for u in at_step[s]:
                                unit(a[0], u)
                            if s == SPREAD:
                                maxima(a[0])
                            if s == MAX_STEP:
                                max_rows(a[0])
                        if s - 1 in LAST.values():
                            output(n, STEPS[s - 1][0])
                    output(n, NJ - 1)

                iterations(dve, step)


def route(nc, a, d, k, r, ps):
    with ExitStack() as ctx:
        def sb(name, shape, dt=F32):
            return ctx.enter_context(nc.sbuf_tensor(name, shape, dt))

        def sem(name):
            return ctx.enter_context(nc.semaphore("r_" + name))

        o_t = sb("o_t", [P, 2, NG, BLK])
        x_in, x_mid = sb("x_in", [P, 2, TPB, C]), sb("x_midb", [P, 2, TPB, C])
        rc, yn, y_t = sb("rc", [P, TPB, H]), sb("yn", [P, TPB, C]), sb("y_t", [P, TPB, KC, P])
        stats, mv = sb("stats2", [P, TPB, 6]), sb("mv2", [P, TPB, 2])
        std, rstd = sb("std2", [P, TPB]), sb("rstd2", [P, TPB])
        hn, h2s, h2_t = sb("hn", [P, TPB, C]), sb("h2s", [P, TPB, C]), sb("h2_t", [P, TPB, KC, P])
        lg = sb("lg", [P, TPB, ET])
        top, topi = sb("top", [P, TPB, 8]), sb("topi", [P, TPB, 8], U32)
        o_ld, x_ld = [sem(f"o{j}") for j in range(2)], [sem(f"x{j}") for j in range(2)]
        ta_done, rc_step, yn_done, tb_done, yt_done, out_done = (sem(n) for n in ("ta", "rc", "yn", "tb", "yt", "out"))
        norm_step, std_done, hn_done, mod_step, tc_done, ht_done, h2c_done, lg_done, top_step = (
            sem(n) for n in ("norm", "std", "hn", "mod", "tc", "ht", "h2c", "lg", "top"))
        x_st = [sem(f"xs{j}") for j in range(2)]
        pa, pb, pc, pd = ps[:, 0:2, :], ps[:, 2:4, :], ps[:, 4:6, :], ps[:, 6:8, :]
        pb4 = pb.rearrange("p n (j c t) -> p (n j) c t", j=2, c=KC)
        pc4 = pc.rearrange("p n (j c) -> p (n j) c", j=2)
        pd4 = pd.rearrange("p n (j c t) -> p (n j) c t", j=2, c=KC)
        pl = pd[:, 0, 0:TPB * ET].rearrange("p (j e) -> p j e", j=TPB)
        NORM, TOP = 4, 5
        x_v = a["L0_attn_x"].rearrange("b (n j p) c -> b n p j c", p=P, j=TPB)
        m_v = d["x_mid"].rearrange("(b n j p) c -> b n p j c", p=P, j=TPB, n=BPS)

        with nc.Block() as block:
            @block.sync
            def _(sp):
                sp.sem_inc(ta_done, 2 * TPB)
                sp.sem_inc(rc_step, 2 * 2)
                for s in (yt_done, norm_step, mod_step, h2c_done, tc_done, top_step, x_st[0], x_st[1]):
                    sp.sem_inc(s, 1)

                def load(b, j):
                    par, t = j % 2, BPS * b + j
                    sp.wait_ge(ta_done, TPB * t + TPB)
                    sp.dma_start(o_t[:, par, :, :], d["attn_t"][bass.ds(b, 1), :, :, j * BLK:(j + 1) * BLK].rearrange(
                        "o g p t -> (o p) g t")).then_inc(o_ld[par], 16)
                    sp.dma_start(x_in[:, par, :, :], x_v[bass.ds(b, 1), j].rearrange("o p j c -> (o p) j c")).then_inc(x_ld[par], 16)

                def store(b, j):
                    par, t = j % 2, BPS * b + j
                    sp.wait_ge(norm_step, NORM * t + 1 + 1)
                    apart(sp)
                    sp.dma_start(m_v[bass.ds(b, 1), j].rearrange("o p j c -> (o p) j c"), x_mid[:, par, :, :]).then_inc(x_st[par], 16)

                def ahead(b, j):
                    if isinstance(b, int) and b == 0 and j == 0:
                        load(0, 0)
                    load(b, j) if not (isinstance(b, int) and b == 0 and j == 0) else None

                blocks(sp, load, store)
                for par in range(2):
                    sp.wait_ge(x_st[par], 16 * NB // 2 + 1)

            @block.tensor
            def _(pe):
                def output(b, j):
                    t, par = BPS * b + j, j % 2
                    pe.wait_ge(o_ld[par], 16 * (2 * b + j // 2 + 1))
                    for n in range(TPB):
                        pe.wait_ge(rc_step, 2 * (TPB * t + n) + 2)
                        for g in range(NG):
                            ins = pe.transpose(pa[:, n % 2, g * P:(g + 1) * P], o_t[:, par, g, n * P:(n + 1) * P], k["ident"][:, :])
                        ins.then_inc(ta_done, 1)
                    pe.wait_ge(yt_done, t + 1)
                    for n in range(TPB):
                        pe.wait_ge(rc_step, 2 * (TPB * t + n) + 2 + 4)
                        for c in range(KC):
                            ins = pe.transpose(pb4[:, n, c, :], yn[:, n, c * P:(c + 1) * P], k["ident"][:, :])
                    ins.then_inc(tb_done, 1)
                    pe.wait_ge(yt_done, t + 2)
                    pe.wait_ge(norm_step, NORM * t + 1)
                    for n in range(TPB):
                        for c in range(KC):
                            ins = pe.matmul(pc4[:, n, :], y_t[:, n, c, :], k["wc"][:, bass.ds(b, 1), c, :].rearrange("p o n -> p (o n)"),
                                            start=(c == 0), stop=(c == KC - 1))
                    ins.then_inc(out_done, 1)

                def logits(b, j):
                    t = BPS * b + j
                    pe.wait_ge(mod_step, 2 * t + 2 + 1)
                    pe.wait_ge(top_step, TOP * t + 1)
                    for n in range(TPB):
                        for c in range(KC):
                            ins = pe.transpose(pd4[:, n, c, :], h2s[:, n, c * P:(c + 1) * P], k["ident"][:, :])
                    ins.then_inc(tc_done, 1)
                    pe.wait_ge(ht_done, t + 1)
                    for n in range(TPB):
                        for c in range(KC):
                            ins = pe.matmul(pl[:, n, :], h2_t[:, n, c, :], k["gate"][:, c, :], start=(c == 0), stop=(c == KC - 1))
                    ins.then_inc(lg_done, 1)

                blocks(pe, output, logits)

            @block.vector
            def _(dve):
                def output(b, j):
                    t, par = BPS * b + j, j % 2
                    for n in range(TPB):
                        q = 2 * (TPB * t + n) + 4
                        src = pa[:, n % 2, :].rearrange("p (h s) -> p h s", s=SLOT)
                        dve.wait_ge(ta_done, TPB * t + n + 1 + 2 * TPB)
                        dve.reciprocal(rc[:, n, :], src[:, :, DH]).then_inc(rc_step, 1)
                        dve.wait_ge(rc_step, q + 1)
                        if n == 0:
                            dve.wait_ge(out_done, t) if False else None
                        dve.tensor_tensor(yn[:, n, :].rearrange("p (h s) -> p h s", s=DH), src[:, :, 0:DH],
                                          wide(rc[:, n, :, None], 2, DH), ALU.mult).then_inc(rc_step, 1)
                    dve.wait_ge(out_done, t + 1)
                    dve.wait_ge(x_ld[par], 16 * (2 * b + j // 2 + 1))
                    dve.wait_ge(x_st[par], 16 * (2 * b + j // 2) + 1)
                    at = NORM * t + 1
                    dve.tensor_tensor(x_mid[:, par, :, :], pc4, x_in[:, par, :, :], ALU.add).then_inc(norm_step, 1)
                    dve.wait_ge(norm_step, at + 1)
                    for n in range(TPB):
                        ins = dve.bn_stats(stats[:, n, :], x_mid[:, par, n, :])
                    ins.then_inc(norm_step, 1)
                    dve.wait_ge(norm_step, at + 2)
                    apart(dve)
                    for n in range(TPB):
                        ins = dve.bn_aggr(mv[:, n, :], stats[:, n, :])
                    ins.then_inc(norm_step, 1)
                    dve.wait_ge(std_done, t + 1)
                    dve.reciprocal(rstd[:, :], std[:, :]).then_inc(norm_step, 1)
                    dve.wait_ge(norm_step, at + 4)
                    dve.wait_ge(mod_step, 2 * t + 1)
                    for n in range(TPB):
                        ins = dve.tensor_scalar(hn[:, n, :], x_mid[:, par, n, :], mv[:, n, 0:1], rstd[:, n:n + 1],
                                                ALU.subtract, ALU.mult)
                    ins.then_inc(hn_done, 1)

                def top2(b, j):
                    t = BPS * b + j
                    at = TOP * t + 1
                    dve.wait_ge(lg_done, t + 1)
                    dve.tensor_tensor(lg[:, :, :], pl, wide(k["bias"][:, None, :], 1, TPB), ALU.add).then_inc(top_step, 1)
                    dve.wait_ge(top_step, at + 1)
                    apart(dve)
                    for n in range(TPB):
                        ins = dve.max(top[:, n, :], lg[:, n, :])
                    ins.then_inc(top_step, 1)
                    dve.wait_ge(top_step, at + 2)
                    apart(dve)
                    for n in range(TPB):
                        ins = dve.max_index(topi[:, n, :], top[:, n, :], lg[:, n, :])
                    ins.then_inc(top_step, 1)
                    dve.wait_ge(top_step, at + 3)
                    dve.tensor_copy(r["top2"][:, bass.ds(TPB * t, TPB), :], top[:, :, 0:2]).then_inc(top_step, 1)
                    dve.tensor_copy(r["idx2"][:, bass.ds(TPB * t, TPB), :], topi[:, :, 0:2]).then_inc(top_step, 1)
                    dve.wait_ge(top_step, at + 5)

                blocks(dve, output, top2)

            @block.scalar
            def _(act):
                def output(b, j):
                    t = BPS * b + j
                    act.wait_ge(tb_done, t + 1)
                    act.copy(y_t[:, :, :, :], pb4).then_inc(yt_done, 1)
                    act.wait_ge(norm_step, NORM * t + 1 + 3)
                    act.activation(std[:, :], mv[:, :, 1], ACT.Sqrt, bias=k["eps"][:, :]).then_inc(std_done, 1)

                def logits(b, j):
                    t = BPS * b + j
                    act.wait_ge(tc_done, t + 1 + 1)
                    act.copy(h2_t[:, :, :, :], pd4).then_inc(ht_done, 1)
                    act.copy(r["h2"][:, bass.ds(TPB * t, TPB), :], h2s[:, :, :]).then_inc(h2c_done, 1)

                blocks(act, output, logits)

            @block.gpsimd
            def _(pool):
                def modulate(b, j):
                    t = BPS * b + j
                    pool.wait_ge(hn_done, t + 1)
                    pool.wait_ge(tc_done, t + 1)
                    pool.wait_ge(h2c_done, t + 1)
                    apart(pool)
                    for q, op in ((1, ALU.mult), (0, ALU.add)):
                        row = wide(k["sbc"][:, bass.ds(b, 1), q, :], 1, TPB)
                        pool.tensor_tensor(h2s[:, :, :], hn[:, :, :] if q else h2s[:, :, :], row, op).then_inc(mod_step, 1)
                        if q:
                            pool.wait_ge(mod_step, 2 * t + 1 + 1)
                            apart(pool)

                def nothing(b, j):
                    pass

                blocks(pool, modulate, nothing)


def place(nc, a, d, k, r, w, ps):
    with ExitStack() as ctx:
        def sb(name, shape, dt=F32):
            return ctx.enter_context(nc.sbuf_tensor(name, shape, dt))

        def sem(name):
            return ctx.enter_context(nc.semaphore("l_" + name))

        consts = {n: sb(n, s) for n, s in {"tri": [P, P], "ones": [P, P], "iota_e": [P, ET], "iota_t": [P, NSLOT_T],
                                           "spare": [P, NT]}.items()}
        idxf, oh, ohs = sb("idxf", [P, NT, 2]), sb("oh", [P, 2, NT, ET]), sb("ohs", [P, NT, E])
        cum, rank = sb("cum", [P, 2, NT, E]), sb("rank", [P, NT, E])
        cnt, cnt_i, base, tend = sb("cnt", [P, E]), sb("cnt_i", [P, E], I32), sb("base", [P, E]), sb("tend", [P, E])
        sel, zero, posf = sb("sel", [P, NT, E]), sb("zerof", [P, 2, NT]), sb("posf", [P, NT])
        dif, wtmp = sb("dif", [P, NT]), sb("wtmp", [P, NT])
        cmp, eidf = sb("cmp", [P, NSLOT_T, E]), sb("eidf", [P, NSLOT_T])
        w_in = sb("w_in", [P, 2, FC * C])
        c_ld, step, w_dif, w_sig, cnt_mm, pos_done, scat, tr_done, tr_copy = (
            sem(n) for n in ("c", "step", "dif", "sig", "cnt", "pos", "scat", "tr", "trc"))
        w_ld = [sem(f"w{j}") for j in range(2)]
        NW = 2 * E

        with nc.Block() as block:
            @block.sync
            def _(sp):
                sp.sem_inc(tr_done, 4)
                sp.sem_inc(tr_copy, 2)
                for n in consts:
                    sp.dma_start(consts[n][:, :], a[n]).then_inc(c_ld, 16)
                w1_v = a["L0_ffn_w1"].rearrange("e (f p) c -> e p f c", p=P)
                w2_v = a["L0_ffn_w2"].rearrange("e (c p) f -> e p c f", p=P)
                with sp.Fori(0, E) as e:
                    sp.wait_ge(tr_done, 4 * e + 2)
                    sp.dma_start(w_in[:, 0, :].rearrange("p (f c) -> p f c", f=FC),
                                 w1_v[bass.ds(e, 1)].rearrange("o p f c -> (o p) f c")).then_inc(w_ld[0], 16)
                    sp.wait_ge(tr_done, 4 * e + 4)
                    sp.dma_start(w_in[:, 1, :].rearrange("p (c f) -> p c f", c=KC),
                                 w2_v[bass.ds(e, 1)].rearrange("o p c f -> (o p) c f")).then_inc(w_ld[1], 16)

            @block.tensor
            def _(pe):
                pe.wait_ge(c_ld, 16 * len(consts))
                pe.wait_ge(step, 5)
                pe.matmul(ps[:, 0, :], consts["tri"][:, :], ohs[:, :, :].rearrange("p t e -> p (t e)"), start=True, stop=True)
                pe.matmul(ps[:, 1, :], consts["ones"][:, :], ohs[:, :, :].rearrange("p t e -> p (t e)"),
                          start=True, stop=True).then_inc(cnt_mm, 1)
                with pe.Fori(0, E) as e:
                    for half in range(4):
                        m, h = half // 2, half % 2
                        if h == 0:
                            pe.wait_ge(w_ld[m], 16 * e + 16)
                        pe.wait_ge(tr_copy, 4 * e + half + 1)
                        for q in range(4):
                            at = (q * KC + h) * P if m == 0 else ((q % 2) * FC + 2 * h + q // 2) * P
                            ins = pe.transpose(ps[:, 2 + half % 2, q * P:(q + 1) * P], w_in[:, m, at:at + P], k["ident"][:, :])
                        ins.then_inc(tr_done, 1)

            @block.scalar
            def _(act):
                act.wait_ge(w_dif, 1)
                act.activation(r["w12"][:, :, 0], dif[:, :], ACT.Sigmoid)
                act.activation(r["w12"][:, :, 1], dif[:, :], ACT.Sigmoid, scale=-1.0).then_inc(w_sig, 1)
                with act.Fori(0, E) as e:
                    for half in range(4):
                        m, h = half // 2, half % 2
                        act.wait_ge(tr_done, 4 * e + half + 1 + 4)
                        src = ps[:, 2 + half % 2, :]
                        if m == 0:
                            dst = w["w1t"][:, bass.ds(e, 1), h, :].rearrange("p o f -> p (o f)")
                        else:
                            dst = w["w2t"][:, bass.ds(e, 1), 2 * h:2 * h + 2, :].rearrange("p o f c -> p (o f c)")
                        act.copy(dst, src).then_inc(tr_copy, 1)

            @block.vector
            def _(dve):
                s = Steps(dve, step)
                dve.wait_ge(c_ld, 16 * len(consts))
                dve.tensor_tensor(dif[:, :], r["top2"][:, :, 0], r["top2"][:, :, 1], ALU.subtract).then_inc(w_dif, 1)
                s.link(dve.tensor_copy(idxf[:, :, :], r["idx2"][:, :, :]))
                for c in range(2):
                    s.link(dve.tensor_tensor(oh[:, c, :, :], wide(idxf[:, :, c:c + 1], 2, ET),
                                             wide(consts["iota_e"][:, None, :], 1, NT), ALU.is_equal))
                s.link(dve.tensor_tensor(ohs[:, :, :], oh[:, 0, :, 0:E], oh[:, 1, :, 0:E], ALU.add))
                s.link(dve.memset(base[:, :], 0.0))
                for c in range(2):
                    s.link(dve.tensor_reduce(zero[:, c, :], oh[:, c, :, E:ET], AX_X, ALU.add))
                dve.wait_ge(w_sig, 1)
                s.link(dve.tensor_tensor(r["wz"][:, :], zero[:, 0, :], r["w12"][:, :, 0], ALU.mult))
                s.link(dve.tensor_tensor(wtmp[:, :], zero[:, 1, :], r["w12"][:, :, 1], ALU.mult))
                s.link(dve.tensor_tensor(r["wz"][:, :], r["wz"][:, :], wtmp[:, :], ALU.add))
                dve.wait_ge(cnt_mm, 1)
                s.link(dve.tensor_copy(rank[:, :, :], ps[:, 0, :]))
                s.link(dve.tensor_copy(cum[:, 0, :, :], ps[:, 1, :]))
                s.link(dve.tensor_tensor(rank[:, :, :], rank[:, :, :], cum[:, 0, :, :], ALU.subtract))
                src, sh = 0, 1
                while sh < NT:
                    s.mark(dve.tensor_copy(cum[:, 1 - src, 0:sh, :], cum[:, src, 0:sh, :]))
                    s.link(dve.tensor_tensor(cum[:, 1 - src, sh:, :], cum[:, src, sh:, :], cum[:, src, 0:NT - sh, :], ALU.add))
                    src, sh = 1 - src, 2 * sh
                s.link(dve.tensor_tensor(rank[:, :, :], rank[:, :, :], cum[:, src, :, :], ALU.add))
                s.link(dve.tensor_scalar(cnt[:, :], cum[:, src, NT - 1, :], float(P - 1), None, ALU.add))
                s.link(dve.tensor_copy(cnt_i[:, :], cnt[:, :]))
                s.link(dve.tensor_scalar(cnt_i[:, :], cnt_i[:, :], 7, None, ALU.arith_shift_right))
                s.link(dve.tensor_copy(cnt[:, :], cnt_i[:, :]))
                for e in range(1, E):
                    s.link(dve.tensor_tensor(base[:, e:e + 1], base[:, e - 1:e], cnt[:, e - 1:e], ALU.add))
                s.link(dve.tensor_tensor(tend[:, :], base[:, :], cnt[:, :], ALU.add))
                s.link(dve.tensor_scalar(base[:, :], base[:, :], float(P), None, ALU.mult))
                s.link(dve.tensor_tensor(rank[:, :, :], rank[:, :, :], wide(base[:, None, :], 1, NT), ALU.add))
                for c in range(2):
                    s.link(dve.tensor_tensor(sel[:, :, :], rank[:, :, :], oh[:, c, :, 0:E], ALU.mult))
                    s.link(dve.tensor_reduce(posf[:, :], sel[:, :, :], AX_X, ALU.add))
                    s.link(dve.scalar_tensor_tensor(wtmp[:, :], consts["spare"][:, :], float(c), zero[:, c, :], ALU.add, ALU.mult))
                    s.link(dve.tensor_tensor(posf[:, :], posf[:, :], wtmp[:, :], ALU.add))
                    s.link(dve.tensor_copy(r["pos"][c][:, :], posf[:, :]))
                    dve.nop().then_inc(pos_done, 1)
                    s.link(dve.tensor_scalar(posf[:, :], posf[:, :], float(ZROW), None, ALU.min))
                    s.link(dve.tensor_copy(r["gpos"][c][:, :], posf[:, :]))
                s.link(dve.tensor_tensor(cmp[:, :, :], wide(tend[:, None, :], 1, NSLOT_T),
                                         wide(consts["iota_t"][:, :, None], 2, E), ALU.is_le))
                s.link(dve.tensor_reduce(eidf[:, :], cmp[:, :, :], AX_X, ALU.add))
                s.link(dve.tensor_scalar(eidf[:, :], eidf[:, :], float(E - 1), None, ALU.min))
                s.link(dve.tensor_copy(w["eid"][:, :], eidf[:, :]))

            @block.gpsimd
            def _(pool):
                for c in range(2):
                    pool.wait_ge(pos_done, c + 1)
                    for t in range(NT):
                        pool.indirect_dma_start(d["slot_x"][:, :], bass.IndirectOffsetOnAxis(ap=r["pos"][c][:, t:t + 1], axis=0),
                                                r["h2"][:, t, :], None).then_inc(scat, 16)
                pool.wait_ge(scat, 16 * 2 * NT)


def experts(nc, d, k, w, ps):
    with ExitStack() as ctx:
        def sb(name, shape, dt=F32):
            return ctx.enter_context(nc.sbuf_tensor(name, shape, dt))

        def sem(name):
            return ctx.enter_context(nc.semaphore("e_" + name))

        xs, ys = sb("xs", [P, 2, C]), sb("ys", [P, 2, C])
        x_t, hid, h_t = sb("x_t", [P, KC, P]), sb("hid", [P, F]), sb("hid_t", [P, FC, P])
        x_ld, y_st = [sem(f"x{j}") for j in range(2)], [sem(f"y{j}") for j in range(2)]
        tx_done, xt_done, up_done, silu_done, th_done, ht_done, down_done, y_done = (
            sem(n) for n in ("tx", "xt", "up", "silu", "th", "ht", "down", "y"))
        px, ph, pt, py = (ps[:, n, :] for n in range(4))
        N = NSLOT_T
        xv = d["slot_x"][0:NSLOT, :].rearrange("(n p) c -> n p c", p=P)
        yv = d["slot_y"][0:NSLOT, :].rearrange("(n p) c -> n p c", p=P)

        with nc.Block() as block:
            @block.sync
            def _(sp):
                sp.sem_inc(y_done, 1)
                for q in range(2):
                    sp.sem_inc(y_st[q], 1)

                def load(t, q):
                    sp.dma_start(xs[:, q, :], xv[bass.ds(t, 1)].rearrange("o p c -> (o p) c")).then_inc(x_ld[q], 16)

                def store(t, q):
                    sp.wait_ge(y_done, t + 2)
                    sp.dma_start(yv[bass.ds(t, 1)].rearrange("o p c -> (o p) c"), ys[:, q, :]).then_inc(y_st[q], 16)

                load(0, 0)
                load(1, 1)
                with sp.Fori(0, N // 2 - 1) as i:
                    for q in range(2):
                        sp.wait_ge(tx_done, 2 * i + q + 1)
                        load(2 * i + q + 2, q)
                        store(2 * i + q, q)
                for q in range(2):
                    store(N - 2 + q, q)
                for q in range(2):
                    sp.wait_ge(y_st[q], 16 * N // 2 + 1)

            @block.tensor
            def _(pe):
                def expert(t):
                    return pe.value_load(w["eid"][0:1, bass.ds(t, 1)], min_val=0, max_val=E - 1)

                def turn_x(t, q, i):
                    pe.wait_ge(x_ld[q], 16 * i + 16)
                    for c in range(KC):
                        ins = pe.transpose(px[:, c * P:(c + 1) * P], xs[:, q, c * P:(c + 1) * P], k["ident"][:, :])
                    ins.then_inc(tx_done, 1)

                def up(t):
                    e = expert(t)
                    pe.wait_ge(xt_done, t + 1)
                    for c in range(KC):
                        ins = pe.matmul(ph, x_t[:, c, :], w["w1t"][:, bass.ds(e, 1), c, :].rearrange("p o f -> p (o f)"),
                                        start=(c == 0), stop=(c == KC - 1))
                    ins.then_inc(up_done, 1)

                def turn_h(t):
                    pe.wait_ge(silu_done, t + 1)
                    for f in range(FC):
                        ins = pe.transpose(pt[:, f * P:(f + 1) * P], hid[:, f * P:(f + 1) * P], k["ident"][:, :])
                    ins.then_inc(th_done, 1)

                def down(t):
                    e = expert(t)
                    pe.wait_ge(ht_done, t + 1)
                    pe.wait_ge(y_done, t + 1)
                    for f in range(FC):
                        ins = pe.matmul(py[:, 0:C], h_t[:, f, :], w["w2t"][:, bass.ds(e, 1), f, :].rearrange("p o c -> p (o c)"),
                                        start=(f == 0), stop=(f == FC - 1))
                    ins.then_inc(down_done, 1)

                turn_x(0, 0, 0)
                up(0)
                turn_x(1, 1, 0)
                with pe.Fori(0, N // 2 - 1) as i:
                    for q in range(2):
                        t = 2 * i + q
                        turn_h(t)
                        up(t + 1)
                        down(t)
                        turn_x(t + 2, q, i + 1)
                turn_h(N - 2)
                up(N - 1)
                down(N - 2)
                turn_h(N - 1)
                down(N - 1)

            @block.scalar
            def _(act):
                with act.Fori(0, N) as t:
                    act.wait_ge(up_done, t + 1)
                    act.activation(hid[:, :], ph, ACT.Silu).then_inc(silu_done, 1)

            @block.vector
            def _(dve):
                def copy_x(t):
                    dve.wait_ge(tx_done, t + 1)
                    dve.tensor_copy(x_t[:, :, :], px[:, 0:C]).then_inc(xt_done, 1)

                def copy_h(t):
                    dve.wait_ge(th_done, t + 1)
                    dve.tensor_copy(h_t[:, :, :], pt).then_inc(ht_done, 1)

                def copy_y(t, q, i):
                    dve.wait_ge(down_done, t + 1)
                    dve.wait_ge(y_st[q], 16 * i + 1)
                    dve.tensor_copy(ys[:, q, :], py[:, 0:C]).then_inc(y_done, 1)

                copy_x(0)
                copy_x(1)
                with dve.Fori(0, N // 2 - 1) as i:
                    for q in range(2):
                        t = 2 * i + q
                        copy_h(t)
                        copy_y(t, q, i)
                        copy_x(t + 2)
                for q in range(2):
                    copy_h(N - 2 + q)
                    copy_y(N - 2 + q, q, N // 2 - 1)


def combine(nc, d, k, r, out):
    with ExitStack() as ctx:
        def sb(name, shape, dt=F32):
            return ctx.enter_context(nc.sbuf_tensor(name, shape, dt))

        def sem(name):
            return ctx.enter_context(nc.semaphore("c_" + name))

        R = 4
        y = sb("y_in", [P, 2, R, C])
        xm, acc = sb("xm", [P, 2, R, C]), sb("acc", [P, 2, R, C])
        g_ld = [[sem(f"g{c}{q}") for q in range(R)] for c in range(2)]
        x_ld, o_st = [sem(f"x{q}") for q in range(2)], [sem(f"o{q}") for q in range(2)]
        used, step, done = sem("used"), sem("step"), sem("done")
        NGRP = NT // R
        ACC = 3
        xv = d["x_mid"].rearrange("(n j p) c -> n p j c", p=P, j=R)
        ov = out.rearrange("b (n j p) c -> (b n) p j c", p=P, j=R)

        with nc.Block() as block:
            @block.gpsimd
            def _(pool):
                for t in range(NT):
                    if t >= R:
                        pool.wait_ge(used, t - R + 1)
                    for c in range(2):
                        pool.indirect_dma_start(y[:, c, t % R, :], None, d["slot_y"][:, :],
                                                bass.IndirectOffsetOnAxis(ap=r["gpos"][c][:, t:t + 1], axis=0)).then_inc(g_ld[c][t % R], 16)

            @block.sync
            def _(sp):
                def load(n, q):
                    sp.dma_start(xm[:, q, :, :], xv[bass.ds(n, 1)].rearrange("o p j c -> (o p) j c")).then_inc(x_ld[q], 16)

                def store(n, q):
                    sp.wait_ge(done, n + 1)
                    sp.dma_start(ov[bass.ds(n, 1)].rearrange("o p j c -> (o p) j c"), acc[:, q, :, :]).then_inc(o_st[q], 16)

                for q in range(2):
                    sp.sem_inc(o_st[q], 1)
                    load(q, q)
                with sp.Fori(0, NGRP // 2 - 1) as i:
                    for q in range(2):
                        store(2 * i + q, q)
                        load(2 * i + q + 2, q)
                for q in range(2):
                    store(NGRP - 2 + q, q)
                for q in range(2):
                    sp.wait_ge(o_st[q], 16 * NGRP // 2 + 1)

            @block.vector
            def _(dve):
                GPS = NGRP // B
                with dve.Fori(0, B) as b:
                    for j in range(GPS):
                        g, q, i = GPS * b + j, j % 2, GPS // 2 * b + j // 2
                        at = (ACC * R + 1) * g
                        dve.wait_ge(o_st[q], 16 * i + 1)
                        for n in range(R):
                            o, t = acc[:, q, n, :], R * g + n
                            dve.wait_ge(g_ld[0][n], 16 * g + 16)
                            dve.tensor_scalar(o, y[:, 0, n, :], r["w12"][:, bass.ds(t, 1), 0], None, ALU.mult).then_inc(step, 1)
                            dve.wait_ge(step, at + 3 * n + 1)
                            dve.wait_ge(g_ld[1][n], 16 * g + 16)
                            dve.scalar_tensor_tensor(o, y[:, 1, n, :], r["w12"][:, bass.ds(t, 1), 1], o, ALU.mult,
                                                     ALU.add).then_inc(step, 1)
                            dve.wait_ge(step, at + 3 * n + 2)
                            dve.scalar_tensor_tensor(o, r["h2"][:, bass.ds(t, 1), :].rearrange("p o c -> p (o c)"),
                                                     r["wz"][:, bass.ds(t, 1)], o, ALU.mult, ALU.add).then_inc(step, 1)
                            dve.wait_ge(step, at + 3 * n + 3)
                            dve.nop().then_inc(used, 1)
                        gb = wide(k["gb"][:, bass.ds(b, 1), :], 1, R)
                        dve.tensor_tensor(acc[:, q, :, :], acc[:, q, :, :], gb, ALU.mult).then_inc(step, 1)
                        dve.wait_ge(step, at + ACC * R + 1)
                        dve.wait_ge(x_ld[q], 16 * i + 16)
                        dve.tensor_tensor(acc[:, q, :, :], acc[:, q, :, :], xm[:, q, :, :], ALU.add).then_inc(done, 1)


_INS = ["L0_attn_x", "L0_attn_Wq_down", "L0_attn_Wk_down", "L0_attn_Wv_down", "L0_attn_Wq_up_c", "L0_attn_Wq_up_e",
        "L0_attn_Wk_up_c", "L0_attn_Wk_up_e", "L0_attn_Wv_up", "L0_attn_Wc", "L0_ffn_gate_w", "L0_ffn_expert_bias",
        "L0_ffn_w1", "L0_ffn_w2", "L0_c", "L0_wmod"]


def constants():
    p = np.arange(P)
    eye = np.eye(P, dtype=np.float32)
    above = np.where(p[None, :] > p[:, None], np.float32(-BIG), np.float32(0))
    half = DH // 2
    inv = np.float32(1.0) / np.float32(10000.0) ** (np.arange(0, half, 2, dtype=np.float32) / np.float32(half))
    ang = np.arange(T, dtype=np.float32)[:, None] * inv[None, :].astype(np.float32)
    ang = np.concatenate([ang, ang], axis=1).astype(np.float32)
    cos = np.ones((T, DH), np.float32)
    sin = np.zeros((T, DH), np.float32)
    cos[:, half:] = np.cos(ang)
    sin[:, half:] = np.sin(ang) * np.where(np.arange(half) % 2 == 0, -1, 1).astype(np.float32)
    return {
        "ident": eye, "mask_qk": above, "mask_kq": above.T.copy(),
        "cos": np.tile(cos.T, (P // DH, 1)).copy(), "sin": np.tile(sin.T, (P // DH, 1)).copy(),
        "tri": (p[:, None] < p[None, :]).astype(np.float32), "ones": np.ones((P, P), np.float32),
        "iota_e": np.tile(np.arange(ET, dtype=np.float32), (P, 1)),
        "iota_t": np.tile(np.arange(NSLOT_T, dtype=np.float32), (P, 1)),
        "spare": (NSLOT + 2 * (P * np.arange(NT)[None, :] + p[:, None])).astype(np.float32),
    }


def kernel(**inputs):
    import concourse.bacc as _bacc
    from concourse.bass_utils import run_bass_kernel_spmd as _run

    nc = _bacc.Bacc("TRN2", target_bir_lowering=False, num_devices=1)
    arrays, args = {}, {}
    given = {n: np.ascontiguousarray(inputs[n]) for n in _INS}
    for name, x in {**given, **constants()}.items():
        arrays[f"in_{name}"] = x
        args[name] = nc.dram_tensor(f"in_{name}", x.shape, mybir.dt.from_np(x.dtype), kind="ExternalInput").ap()
    out = nc.dram_tensor("out_0", (B, T, C), F32, kind="ExternalOutput").ap()
    build(nc, args, out)
    r = _run(nc, [arrays], core_ids=[0])
    return r.results[0]["out_0"]
```

```python
from contextlib import ExitStack

import numpy as np

import concourse.bass as bass
from concourse import mybir

ALU = mybir.AluOpType
ACT = mybir.ActivationFunctionType
F32 = mybir.dt.float32
BF16 = mybir.dt.bfloat16
I32 = mybir.dt.int32
U32 = mybir.dt.uint32
AX_X = mybir.AxisListType.X

P = 128
B, T, C = 4, 2048, 256
H, L, DH = 16, 64, 16
KC = C // P
NTOK = B * T
NT = NTOK // P
TT = T // P
BLK = 512
NB = NTOK // BLK
TPB = BLK // P
BPS = T // BLK
EPS = 1e-5
HG = 4
NG = H // HG
NIT = B * NG
SLOT = 32
QB = 256
NJ = T // QB
COMBOS = [(0, 0), (0, 1), (1, 0), (1, 1), (0, 2), (2, 0)]
SROWS = 16 * len(COMBOS)
MROWS = 3
E, EZ, F = 8, 4, 512
ET = E + EZ
FC = F // P
NSLOT_T = 2 * NT + E
NSLOT = NSLOT_T * P
ZROW = NSLOT
BIG = 1e30


def apart(eng):
    eng.nop(nofuse=True)


class Steps:

    def __init__(self, eng, sem):
        self.eng, self.sem, self.base, self.n = eng, sem, 0, 0

    def at(self, base):
        self.base, self.n = base, 0

    def mark(self, ins):
        self.n += 1
        ins.then_inc(self.sem, 1)

    def wait(self):
        self.eng.wait_ge(self.sem, self.base + self.n)

    def link(self, ins):
        self.mark(ins)
        self.wait()


def wide(ap, dim, n):
    shape = list(ap.shape)
    shape[dim] = n
    return ap.broadcast_to(shape)


def staged(eng, *stages):
    def turn(b, j):
        for lag, stage in stages:
            at = (b, j - lag) if j >= lag else (b - 1, j - lag + BPS)
            if not isinstance(b, int) or 0 <= at[0] < B:
                stage(*at)

    for j in range(BPS):
        turn(0, j)
    with eng.Fori(1, B) as b:
        for j in range(BPS):
            turn(b, j)
    for j in range(max(lag for lag, _ in stages)):
        turn(B, j)


def build(nc, a, out):
    d = {}
    with ExitStack() as ctx:
        def dram(name, shape, dt):
            d[name] = nc.dram_tensor(name, shape, dt, kind="Internal").ap()

        dram("q_parts", (3, B, H, DH, T), BF16)
        dram("k_parts", (3, B, H, DH, T), BF16)
        dram("v_ones", (B, NG, P, TT, HG * SLOT), F32)
        dram("attn_t", (B, NG, P, T), F32)
        dram("x_mid", (NTOK, C), F32)
        dram("slot_x", (NSLOT + 2 * P + 2 * NTOK, C), F32)
        dram("slot_y", (NSLOT + P, C), F32)

        def sb(name, shape, dt=F32):
            return ctx.enter_context(nc.sbuf_tensor(name, shape, dt))

        ps = ctx.enter_context(nc.psum_tensor("ps", [P, 8, 512], F32))
        k = {
            "ident": sb("ident", [P, P]),
            "identb": sb("identb", [P, P], BF16),
            "mask_qk": sb("mask_qk", [P, P], BF16),
            "mask_kq": sb("mask_kq", [P, P], BF16),
            "mod": sb("mod", [P, 12, B]),
            "ca1": sb("ca1", [P, KC, B]),
            "sbc": sb("sbc", [P, B, 2, C]),
            "gb": sb("gb", [P, B, C]),
            "wc": sb("wc", [P, B, KC, C]),
            "gate": sb("gate", [P, KC, ET]),
            "bias": sb("bias", [P, ET]),
            "eps": sb("eps", [P, 1]),
        }
        with ExitStack() as c2:
            wf = c2.enter_context(nc.sbuf_tensor("w_fused", [P, 3, KC, C], F32))
            setup(nc, a, k, wf, ps)
            project(nc, a, d, k, wf, ps)
        attention(nc, d, k, ps)
        with ExitStack() as c2:
            r = {n: c2.enter_context(nc.sbuf_tensor(n, s, F32)) for n, s in {
                "h2": [P, NT, C], "w12": [P, NT, 2], "wz": [P, NT], "top2": [P, NT, 2]}.items()}
            r["idx2"] = c2.enter_context(nc.sbuf_tensor("idx2", [P, NT, 2], U32))
            r["pos"] = [c2.enter_context(nc.sbuf_tensor(f"pos{s}", [P, NT], I32)) for s in range(2)]
            r["gpos"] = [c2.enter_context(nc.sbuf_tensor(f"gpos{s}", [P, NT], I32)) for s in range(2)]
            route(nc, a, d, k, r, ps)
            with ExitStack() as c3:
                w = {n: c3.enter_context(nc.sbuf_tensor(n, s, F32)) for n, s in {
                    "w1t": [P, E, KC, F], "w2t": [P, E, FC, C]}.items()}
                w["eid"] = c3.enter_context(nc.sbuf_tensor("eid", [P, NSLOT_T + 2], I32))
                w["npair"] = c3.enter_context(nc.sbuf_tensor("npair", [P, 1], I32))
                place(nc, a, d, k, r, w, ps)
                experts(nc, d, k, w, ps)
            combine(nc, d, k, r, out)


def setup(nc, a, k, wf, ps):
    with ExitStack() as ctx:
        def sb(name, shape, dt=F32):
            return ctx.enter_context(nc.sbuf_tensor(name, shape, dt))

        def sem(name):
            return ctx.enter_context(nc.semaphore(name))

        c_in, c_sig = sb("c_in", [B, C]), sb("c_sig", [B, C])
        gate_in = sb("gate_in", [ET, C])
        down = sb("down", [P, 3, KC, H * L])
        down_t = sb("down_t", [P, 3, H // 2, C])
        up = sb("up", [P, 3, 32])
        wmod = sb("wmod", [P, KC, 6 * C])
        wc_in = sb("wc_in", [P, KC, C])
        c_t = sb("c_t", [P, KC, B])
        masks = sb("masks", [P, 2, P])
        c_rep = sb("c_rep", [P, KC, B, P])
        g_rows = sb("g_rows", [P, B, 2, C])
        g_sign = sb("g_sign", [P, B, 2, C])
        ld_small, ld_down, ld_mod, up_zero, ld_up = (sem(f"s_{n}") for n in ("small", "down", "mod", "upz", "up"))
        sig_done, pe_unit, evac, dve_step = (sem(f"s_{n}") for n in ("sig", "pe", "evac", "dve"))
        downs = ["L0_attn_Wq_down", "L0_attn_Wk_down", "L0_attn_Wv_down"]
        ups = [["L0_attn_Wq_up_c", "L0_attn_Wq_up_e"], ["L0_attn_Wk_up_c", "L0_attn_Wk_up_e"], ["L0_attn_Wv_up"]]
        NSMALL = 7
        NU_DOWN = 2
        NU_MOD = NU_DOWN + 12
        NU_ROWS = NU_MOD + 1
        NU_FUSE = NU_ROWS + 2 * B
        with nc.Block() as block:
            @block.sync
            def _(sp):
                sp.dma_start(c_in[:, :], a["L0_c"]).then_inc(ld_small, 16)
                sp.dma_start(gate_in[:, :], a["L0_ffn_gate_w"]).then_inc(ld_small, 16)
                sp.dma_start(k["ident"][:, :], a["ident"]).then_inc(ld_small, 16)
                sp.dma_start(masks[:, 0, :], a["mask_qk"]).then_inc(ld_small, 16)
                sp.dma_start(masks[:, 1, :], a["mask_kq"]).then_inc(ld_small, 16)
                bias = a["L0_ffn_expert_bias"].rearrange("(o e) -> o e", o=1)
                sp.dma_start(k["bias"][:, :], bias.broadcast_to([P, ET])).then_inc(ld_small, 16)
                sp.dma_start(wc_in[:, :, :], a["L0_attn_Wc"].rearrange("(c p) n -> p c n", p=P)).then_inc(ld_small, 16)
                for x in range(3):
                    sp.dma_start(down[:, x, :, :], a[downs[x]].rearrange("(c p) n -> p c n", p=P)).then_inc(ld_down, 16)
                sp.dma_start(wmod[:, :, :], a["L0_wmod"].rearrange("(c p) n -> p c n", p=P)).then_inc(ld_mod, 16)
                sp.wait_ge(up_zero, 1)
                for x in range(3):
                    for half in range(2):
                        for n, name in enumerate(ups[x]):
                            w = DH // len(ups[x])
                            sp.dma_start(up[half * L:(half + 1) * L, x, half * DH + n * w:half * DH + (n + 1) * w],
                                         a[name]).then_inc(ld_up, 16)

            @block.scalar
            def _(act):
                act.wait_ge(ld_small, 16 * NSMALL)
                act.activation(c_sig[:, :], c_in[:, :], ACT.Sigmoid).then_inc(sig_done, 1)

            @block.tensor
            def _(pe):
                unit = [0]

                def begin():
                    if unit[0] >= 8:
                        pe.wait_ge(evac, unit[0] - 7)
                    return ps[:, unit[0] % 8, :]

                def end(ins):
                    unit[0] += 1
                    ins.then_inc(pe_unit, 1)

                pe.wait_ge(dve_step, 1)
                o = begin()
                for c in range(KC):
                    ins = pe.transpose(o[:, B * c:B * c + B], c_in[:, c * P:(c + 1) * P], k["ident"][0:B, 0:B])
                end(ins)
                o = begin()
                for c in range(KC):
                    ins = pe.transpose(o[:, ET * c:ET * c + ET], gate_in[:, c * P:(c + 1) * P], k["ident"][0:ET, 0:ET])
                end(ins)
                pe.wait_ge(ld_down, 48)
                for x in range(3):
                    for pp in range(H // 4):
                        o = begin()
                        for q in range(2):
                            for c in range(KC):
                                pair = 2 * pp + q
                                ins = pe.transpose(o[:, (q * KC + c) * P:(q * KC + c + 1) * P],
                                                   down[:, x, c, pair * P:(pair + 1) * P], k["ident"][:, :])
                        end(ins)
                pe.wait_ge(ld_mod, 16)
                pe.wait_ge(evac, 1)
                o = begin()
                for j in range(12):
                    for c in range(KC):
                        ins = pe.matmul(o[:, j * B:(j + 1) * B], wmod[:, c, j * P:(j + 1) * P], c_t[:, c, :],
                                        start=(c == 0), stop=(c == KC - 1))
                end(ins)
                pe.wait_ge(dve_step, 2)
                for first, second in ((2, 5), (3, 4)):
                    for b in range(B):
                        o = begin()
                        for n, g in enumerate((first, second)):
                            for c in range(KC):
                                ins = pe.matmul(o[:, n * C:(n + 1) * C], c_rep[:, c, b, :], wmod[:, c, g * C:(g + 1) * C],
                                                start=(c == 0), stop=(c == KC - 1))
                        end(ins)
                pe.wait_ge(ld_up, 16 * 10)
                pe.wait_ge(evac, NU_MOD)
                for x in range(3):
                    o = begin()
                    for c in range(KC):
                        for pair in range(H // 2):
                            at = c * C + 32 * pair
                            ins = pe.matmul(o[:, at:at + 32], down_t[:, x, pair, c * P:(c + 1) * P], up[:, x, :],
                                            start=True, stop=True)
                    end(ins)

            @block.vector
            def _(dve):
                unit = [0]

                def begin():
                    dve.wait_ge(pe_unit, unit[0] + 1)
                    o = ps[:, unit[0] % 8, :]
                    unit[0] += 1
                    return o

                dve.memset(up[:, :, :], 0.0).then_inc(up_zero, 1)
                dve.memset(k["eps"][:, :], EPS)
                dve.wait_ge(sig_done, 1)
                dve.tensor_tensor(c_in[:, :], c_in[:, :], c_sig[:, :], ALU.mult).then_inc(dve_step, 1)
                dve.tensor_copy(c_t[:, :, :], begin()[:, 0:KC * B]).then_inc(evac, 1)
                dve.wait_ge(evac, 1)
                dve.tensor_copy(c_rep[:, :, :, :], wide(c_t[:, :, :, None], 3, P)).then_inc(dve_step, 1)
                dve.tensor_copy(k["gate"][:, :, :], begin()[:, 0:KC * ET]).then_inc(evac, 1)
                for x in range(3):
                    for pp in range(H // 4):
                        dve.tensor_copy(down_t[:, x, 2 * pp:2 * pp + 2, :], begin()[:, :]).then_inc(evac, 1)
                dve.tensor_copy(k["mod"][:, :, :], begin()[:, 0:12 * B]).then_inc(evac, 1)
                for b in range(B):
                    dve.tensor_copy(g_rows[:, b, :, :], begin()[:, :]).then_inc(evac, 1)
                for b in range(B):
                    o = begin()
                    dve.tensor_copy(k["sbc"][:, b, 0, :], o[:, 0:C])
                    dve.tensor_scalar(k["sbc"][:, b, 1, :], o[:, C:2 * C], 1.0, None, ALU.add).then_inc(evac, 1)
                dve.wait_ge(evac, NU_FUSE)
                dve.tensor_copy(k["identb"][:, :], k["ident"][:, :])
                dve.tensor_copy(k["mask_qk"][:, :], masks[:, 0, :])
                dve.tensor_copy(k["mask_kq"][:, :], masks[:, 1, :])
                dve.tensor_scalar(k["ca1"][:, :, :], k["mod"][:, 2:4, :], 1.0, None, ALU.add).then_inc(dve_step, 1)
                dve.tensor_scalar(g_sign[:, :, :, :], g_rows[:, :, :, :], 0.0, 2.0, ALU.is_ge, ALU.mult).then_inc(dve_step, 1)
                dve.wait_ge(dve_step, 4)
                dve.tensor_scalar(g_sign[:, :, :, :], g_sign[:, :, :, :], -1.0, None, ALU.add).then_inc(dve_step, 1)
                dve.wait_ge(dve_step, 5)
                dve.tensor_tensor(g_rows[:, :, :, :], g_rows[:, :, :, :], g_sign[:, :, :, :], ALU.mult).then_inc(dve_step, 1)
                dve.wait_ge(dve_step, 6)
                dve.tensor_scalar(g_rows[:, :, :, :], g_rows[:, :, :, :], 0.25, None, ALU.max).then_inc(dve_step, 1)
                dve.wait_ge(dve_step, 7)
                dve.tensor_tensor(g_rows[:, :, :, :], g_rows[:, :, :, :], g_sign[:, :, :, :], ALU.mult).then_inc(dve_step, 1)
                dve.wait_ge(dve_step, 8)
                dve.tensor_copy(k["gb"][:, :, :], g_rows[:, :, 1, :]).then_inc(dve_step, 1)
                for b in range(B):
                    for c in range(KC):
                        dve.tensor_tensor(k["wc"][:, b, c, :], wc_in[:, c, :], g_rows[:, b, 0, :],
                                          ALU.mult).then_inc(dve_step, 1)
                for x in range(3):
                    dve.tensor_copy(wf[:, x, :, :], begin()[:, :]).then_inc(evac, 1)


def project(nc, a, d, k, wf, ps):
    with ExitStack() as ctx:
        def sb(name, shape, dt=F32):
            return ctx.enter_context(nc.sbuf_tensor(name, shape, dt))

        def sem(name):
            return ctx.enter_context(nc.semaphore("p_" + name))

        NM = H // 8
        X = range(2)
        cos, sin = sb("cos", [P, T]), sb("sin", [P, T])
        xin = sb("xin", [P, BPS, TPB, C])
        stats, mv = sb("stats", [P, TPB, 6]), sb("mv", [P, TPB, 2])
        std, rstd = sb("std", [P, TPB]), sb("rstd", [P, TPB])
        h_t = sb("h_t", [P, 2, KC, BLK])
        raw, rot = sb("raw", [P, 2, 2, NM, BLK]), sb("rot", [P, 2, NM, BLK])
        parts = sb("parts", [P, 2, 3, 2, NM, BLK], BF16)
        vout = sb("vout", [P, 2, TPB, H, SLOT])
        tab_ld, norm_step, std_done, hn_done, tr_done, ht_done, ones_done = (
            sem(n) for n in ("tab", "norm", "std", "hn", "tr", "ht", "ones"))
        qk_done, v_done, copy_done, vcopy_done, rope_step, cos_done, hi_done, mid_done, low_done = (
            sem(n) for n in ("qk", "v", "copy", "vcopy", "rope", "cos", "hi", "mid", "low"))
        x_ld = [sem(f"x{j}") for j in range(BPS)]
        st_parts = [sem(f"stp{j}") for j in range(2)]
        st_v = [sem(f"stv{j}") for j in range(2)]
        x_v = a["L0_attn_x"].rearrange("b (n j p) c -> b n p j c", p=P, j=TPB)
        NPART = 3 * 2 * NM * 16
        NV = TPB * 16
        NORM, ROPE = 3, 8
        hp, qk, vp = ps[:, 0:2, :], ps[:, 2:6, :], ps[:, 6:8, :]

        with nc.Block() as block:
            @block.sync
            def _(sp):
                sp.sem_inc(low_done, 4)
                sp.sem_inc(v_done, 2)
                sp.sem_inc(copy_done, 2)
                for s in (ht_done, vcopy_done, *st_parts, *st_v):
                    sp.sem_inc(s, 1)

                def load(b, j):
                    sp.dma_start(xin[:, j, :, :], x_v[bass.ds(b, 1), j].rearrange("o p j c -> (o p) j c")).then_inc(x_ld[j], 16)

                def store(b, j):
                    par, tok = j % 2, j * BLK
                    sp.wait_ge(vcopy_done, BPS * b + j + 2)
                    for n in range(TPB):
                        dst = d["v_ones"][bass.ds(b, 1), :, :, TPB * j + n, :]
                        sp.dma_start(dst.rearrange("o g p n -> (o p) g n"),
                                     vout[:, par, n, :, :].rearrange("p (g h) s -> p g (h s)", g=NG)).then_inc(st_v[par], 16)
                    sp.wait_ge(low_done, 2 * (BPS * b + j) + 2 + 4)
                    for x, name in enumerate(("q_parts", "k_parts")):
                        for m in range(NM):
                            for part in range(3):
                                dst = d[name][part, bass.ds(b, 1), 8 * m:8 * m + 8, :, tok:tok + BLK]
                                sp.dma_start(dst.rearrange("o h d t -> (o h d) t"),
                                             parts[:, par, part, x, m, :]).then_inc(st_parts[par], 16)

                def sequence(b, last):
                    for j in range(BPS):
                        if not last:
                            sp.wait_ge(tr_done, BPS * b + j + 1)
                            load(b + 1, j)
                        store(b, j)

                for j in range(BPS):
                    load(0, j)
                sp.dma_start(cos[:, :], a["cos"]).then_inc(tab_ld, 16)
                sp.dma_start(sin[:, :], a["sin"]).then_inc(tab_ld, 16)
                with sp.Fori(0, B - 1) as b:
                    sequence(b, False)
                sequence(B - 1, True)
                for par in range(2):
                    sp.wait_ge(st_parts[par], NPART * NB // 2 + 1)
                    sp.wait_ge(st_v[par], NV * NB // 2 + 1)

            @block.vector
            def _(dve):
                def norm(b, j):
                    t = BPS * b + j
                    dve.wait_ge(x_ld[j], 16 * b + 16)
                    for n in range(TPB):
                        ins = dve.bn_stats(stats[:, n, :], xin[:, j, n, :])
                    ins.then_inc(norm_step, 1)
                    dve.wait_ge(norm_step, NORM * t + 1)
                    apart(dve)
                    for n in range(TPB):
                        ins = dve.bn_aggr(mv[:, n, :], stats[:, n, :])
                    ins.then_inc(norm_step, 1)

                def norm_end(b, j):
                    t = BPS * b + j
                    dve.wait_ge(std_done, t + 1)
                    dve.reciprocal(rstd[:, :], std[:, :]).then_inc(norm_step, 1)
                    dve.wait_ge(norm_step, NORM * t + 3)
                    for n in range(TPB):
                        ins = dve.tensor_scalar(xin[:, j, n, :], xin[:, j, n, :], mv[:, n, 0:1],
                                                rstd[:, n:n + 1], ALU.subtract, ALU.mult)
                    ins.then_inc(hn_done, 1)

                def rotate(b, j):
                    t, par, tok = BPS * b + j, j % 2, j * BLK
                    for x in X:
                        dve.wait_ge(copy_done, 2 * t + x + 1 + 2)
                        apart(dve)
                        dve.stream_shuffle(rot[:, x], raw[:, par, x], [r ^ 1 for r in range(32)]).then_inc(rope_step, 1)
                    if isinstance(b, int) and b == 0 and j == 0:
                        dve.wait_ge(tab_ld, 32)
                    for x in X:
                        dve.wait_ge(rope_step, ROPE * t + x + 1)
                        dve.tensor_tensor(rot[:, x], rot[:, x], wide(sin[:, None, tok:tok + BLK], 1, NM),
                                          ALU.mult).then_inc(rope_step, 1)

                def split(b, j):
                    t, par = BPS * b + j, j % 2
                    for x in X:
                        dve.wait_ge(rope_step, ROPE * t + x + 3)
                        dve.wait_ge(cos_done, 2 * t + x + 1)
                        dve.tensor_tensor(raw[:, par, x], raw[:, par, x], rot[:, x], ALU.add).then_inc(rope_step, 1)
                    for x in X:
                        dve.wait_ge(hi_done, 2 * t + x + 1)
                        dve.tensor_tensor(raw[:, par, x], raw[:, par, x], parts[:, par, 0, x], ALU.subtract).then_inc(rope_step, 1)

                staged(dve, (0, norm), (0, norm_end), (2, rotate), (2, split))

            @block.gpsimd
            def _(pool):
                pool.memset(vout[:, :, :, :, :], 1.0).then_inc(ones_done, 1)
                pool.wait_ge(tab_ld, 32)

                def turn(b, j):
                    t, par, tok = BPS * b + j, j % 2, j * BLK
                    for x in X:
                        pool.wait_ge(rope_step, ROPE * t + x + 1)
                        pool.tensor_tensor(raw[:, par, x], raw[:, par, x], wide(cos[:, None, tok:tok + BLK], 1, NM),
                                           ALU.mult).then_inc(cos_done, 1)

                def low(b, j):
                    t, par = BPS * b + j, j % 2
                    for x in X:
                        pool.wait_ge(mid_done, 2 * t + x + 1)
                        pool.tensor_tensor(parts[:, par, 2, x], raw[:, par, x], parts[:, par, 1, x],
                                           ALU.subtract).then_inc(low_done, 1)

                staged(pool, (0, turn), (0, low))

            @block.scalar
            def _(act):
                def norm(b, j):
                    t = BPS * b + j
                    act.wait_ge(norm_step, NORM * t + 2)
                    act.activation(std[:, :], mv[:, :, 1], ACT.Sqrt, bias=k["eps"][:, :]).then_inc(std_done, 1)

                def modulate(b, j):
                    t = BPS * b + j
                    act.wait_ge(tr_done, t + 1)
                    act.wait_ge(v_done, t + 1)
                    apart(act)
                    for c in range(KC):
                        ins = act.activation(h_t[:, j % 2, c, :], hp[:, c, :], ACT.Identity, bias=k["mod"][:, c, bass.ds(b, 1)],
                                             scale=k["ca1"][:, c, bass.ds(b, 1)])
                    ins.then_inc(ht_done, 1)

                def copies(b, j):
                    t, par, n = BPS * b + j, j % 2, 2 * b + j // 2
                    for x in X:
                        act.wait_ge(qk_done, 2 * t + x + 1)
                        act.wait_ge(low_done, 2 * t + x + 1)
                        act.copy(raw[:, par, x], qk[:, NM * x:NM * (x + 1), :]).then_inc(copy_done, 1)
                    act.wait_ge(v_done, t + 3)
                    if isinstance(b, int) and b == 0 and j == 0:
                        act.wait_ge(ones_done, 1)
                    act.wait_ge(st_v[par], NV * n + 1)
                    act.copy(vout[:, par, :, :, 0:DH], vp.rearrange("p n (j h s) -> p (n j) h s", h=H, s=DH)).then_inc(vcopy_done, 1)

                def split(b, j):
                    t, par, n = BPS * b + j, j % 2, 2 * b + j // 2
                    for x in X:
                        act.wait_ge(rope_step, ROPE * t + x + 5)
                        act.wait_ge(st_parts[par], NPART * n + 1)
                        act.copy(parts[:, par, 0, x], raw[:, par, x]).then_inc(hi_done, 1)
                    for x in X:
                        act.wait_ge(rope_step, ROPE * t + x + 7)
                        act.copy(parts[:, par, 1, x], raw[:, par, x]).then_inc(mid_done, 1)

                staged(act, (0, norm), (1, modulate), (2, copies), (2, split))

            @block.tensor
            def _(pe):
                def transposes(b, j):
                    t = BPS * b + j
                    pe.wait_ge(hn_done, t + 1)
                    pe.wait_ge(ht_done, t + 1)
                    for n in range(TPB):
                        for c in range(KC):
                            ins = pe.transpose(hp[:, c, n * P:(n + 1) * P], xin[:, j, n, c * P:(c + 1) * P], k["ident"][:, :])
                    ins.then_inc(tr_done, 1)

                def products(b, j):
                    t, h = BPS * b + j, h_t[:, j % 2]
                    pe.wait_ge(ht_done, t + 2)
                    for x in X:
                        pe.wait_ge(copy_done, 2 * t + x + 1)
                        for m in range(NM):
                            for c in range(KC):
                                ins = pe.matmul(qk[:, NM * x + m, :], wf[:, x, c, m * P:(m + 1) * P], h[:, c, :],
                                                start=(c == 0), stop=(c == KC - 1))
                        ins.then_inc(qk_done, 1)
                    pe.wait_ge(vcopy_done, t + 1)
                    for n in range(TPB):
                        for c in range(KC):
                            ins = pe.matmul(vp[:, n // 2, (n % 2) * C:(n % 2 + 1) * C], h[:, c, n * P:(n + 1) * P],
                                            wf[:, 2, c, :], start=(c == 0), stop=(c == KC - 1))
                    ins.then_inc(v_done, 1)

                staged(pe, (1, transposes), (2, products))


def attention(nc, d, k, ps):
    with ExitStack() as ctx:
        def sb(name, shape, dt=F32):
            return ctx.enter_context(nc.sbuf_tensor(name, shape, dt))

        def sem(name):
            return ctx.enter_context(nc.semaphore("a_" + name))

        R = 3
        NP = 3
        NR = 3
        STEPS = [(J, j) for J in range(NJ) for j in range(QB // P * (J + 1))]
        NS = len(STEPS)
        LAST = {J: max(s for s, (JJ, _) in enumerate(STEPS) if JJ == J) for J in range(NJ)}
        UNITS = [(i, g, c) for i in range(TT) for g in range(HG) for c in range(i // 4 + 1)]
        NUNIT = len(UNITS) + 2
        SPREAD = NS - 10
        cost = np.cumsum([min(512, P * (i + 1) - 512 * c) + 64 for i, _, c in UNITS])
        at_step = [[u for u in range(len(UNITS)) if min(int(cost[u] * SPREAD // cost[-1]), SPREAD - 1) == s] for s in range(NS)]
        MAX_STEP = SPREAD + 1
        NMAX = 9
        ks, qs = sb("ks", [P, R, HG, T], BF16), sb("qs", [P, R, HG, T], BF16)
        vs = sb("vs", [P, R, TT, HG * SLOT])
        probs = sb("probs", [P, NP, HG, QB])
        o_sb = sb("o_sb", [P, 2, QB])
        mxc, negm, res = sb("mxc", [P, HG, TT, 4]), sb("negm", [P, HG, TT]), sb("res", [P, HG, TT])
        mparts = sb("mparts", [P, MROWS, HG * TT], BF16)
        m_t = sb("m_t", [HG * TT, MROWS, P], BF16)
        zero = sb("zero", [P, 8 * C])
        FILL = NIT * 8 * P
        assert FILL <= NSLOT
        ld = [sem(f"ld{r}") for r in range(R)]
        m_ld, init_done, pool_init, red_ready, red_done, max_step, mt_done = (
            sem(n) for n in ("mld", "init", "pinit", "redr", "redd", "max", "mt"))
        st_ready, exp_done, pv_done, o_done, zero_set, zero_st = (sem(n) for n in ("str", "exp", "pv", "o", "zset", "zst"))
        o_st = [sem(f"ost{r}") for r in range(2)]
        LD = 16 * (2 * len(COMBOS) + 1)
        M_LD = 16 * MROWS
        st_ps = ps[:, 0:4, :].rearrange("p (u n) (g q) -> p u (n g) q", u=2, g=2)
        red_ps, o_ps = ps[:, 4:4 + NR, :], ps[:, 7, 0:QB]
        assert NS % 2 == 0 and NS % NP == 0 and NUNIT % NR == 0 and NIT % R == 1

        def iterations(eng, step):
            step((0, 0), None)
            with eng.Fori(0, NIT // R) as i:
                for r in range(R):
                    n = R * i + r
                    step((n + 1, (r + 1) % R), (n, r))
            step(None, (NIT - 1, (NIT - 1) % R))

        with nc.Block() as block:
            @block.sync
            def _(sp):
                sp.sem_inc(red_done, NR)
                sp.sem_inc(exp_done, 2)
                sp.sem_inc(pv_done, NP)
                sp.sem_inc(o_done, 2)
                sp.sem_inc(m_ld, 1)
                for r in range(2):
                    sp.sem_inc(o_st[r], 1)

                qv = d["q_parts"].rearrange("x b (g h) d t -> x (b g) d h t", h=HG)
                kv = d["k_parts"].rearrange("x b (g h) d t -> x (b g) d h t", h=HG)
                vv = d["v_ones"].rearrange("b g p j n -> (b g) p j n")
                ov = d["attn_t"].rearrange("b g p t -> (b g) p t")

                def load(n, r):
                    for m, (kp, qp) in enumerate(COMBOS):
                        sp.dma_start(ks[16 * m:16 * m + 16, r, :, :],
                                     kv[kp, bass.ds(n, 1)].rearrange("o d h t -> (o d) h t")).then_inc(ld[r], 16)
                        sp.dma_start(qs[16 * m:16 * m + 16, r, :, :],
                                     qv[qp, bass.ds(n, 1)].rearrange("o d h t -> (o d) h t")).then_inc(ld[r], 16)
                    sp.dma_start(vs[:, r, :, :], vv[bass.ds(n, 1)].rearrange("o p j n -> (o p) j n")).then_inc(ld[r], 16)

                def maxima(n, r):
                    sp.wait_ge(mt_done, n + 1)
                    for m in range(MROWS):
                        sp.dma_start(qs[SROWS + m:SROWS + m + 1, r, :, :].rearrange("o h (i t) -> o (h i) t", t=P),
                                     m_t[:, m, :]).then_inc(m_ld, 16)

                def step(a, b, more=True):
                    if b is None:
                        return maxima(*a)
                    n, r = b
                    for J in range(NJ):
                        if J == NJ - 1 and a is not None:
                            maxima(*a)
                        sp.wait_ge(o_done, NJ * n + J + 1 + 2)
                        sp.dma_start(ov[bass.ds(n, 1), :, J * QB:(J + 1) * QB].rearrange("o p t -> (o p) t"),
                                     o_sb[:, J % 2, :]).then_inc(o_st[J % 2], 16)
                    if more:
                        load(n + R, r)

                for n in range(R):
                    load(n, n)
                    if n == 0:
                        sp.wait_ge(ld[0], LD)
                step((0, 0), None)
                full = (NIT - R) // R
                with sp.Fori(0, full) as i:
                    for r in range(R):
                        step((R * i + r + 1, (r + 1) % R), (R * i + r, r))
                for n in range(R * full, NIT):
                    step((n + 1, (n + 1) % R) if n + 1 < NIT else None, (n, n % R), n + R < NIT)
                for r in range(2):
                    sp.wait_ge(o_st[r], 16 * NIT * NJ // 2 + 1)

            @block.gpsimd
            def _(pool):
                for r in range(1, R):
                    pool.memset(ks[SROWS:SROWS + MROWS, r, :, :], 1.0).then_inc(pool_init, 1)
                    pool.wait_ge(pool_init, r)
                pool.memset(zero[:, :], 0.0).then_inc(zero_set, 1)
                pool.wait_ge(zero_set, 1)
                fills = [d[n][0:FILL, :].rearrange("(n p r) c -> n p (r c)", p=P, r=8) for n in ("slot_x", "slot_y")]
                with pool.Fori(0, NIT) as i:
                    pool.wait_ge(o_done, NJ * i + 2 + 1)
                    for rows in fills:
                        pool.dma_start(rows[bass.ds(i, 1)].rearrange("o p n -> (o p) n"), zero[:, :]).then_inc(zero_st, 16)
                for n, end in (("slot_x", NSLOT + 2 * P), ("slot_y", NSLOT + P)):
                    for at in range(FILL, end, P):
                        pool.dma_start(d[n][at:at + P, :], zero[:, 0:C]).then_inc(zero_st, 16)
                pool.wait_ge(zero_st, 16 * (2 * NIT + (NSLOT + 2 * P - FILL) // P + (NSLOT + P - FILL) // P))

            @block.tensor
            def _(pe):
                def unit(n, r, u):
                    i, g, c = UNITS[u]
                    w = min(512, P * (i + 1) - 512 * c)
                    diag = c == i // 4
                    o = red_ps[:, u % NR, 0:w]
                    pe.wait_ge(red_done, NUNIT * n + u + 1)
                    ins = pe.matmul(o, qs[0:SROWS, r, g, i * P:(i + 1) * P], ks[0:SROWS, r, g, 512 * c:512 * c + w],
                                    start=True, stop=not diag)
                    if diag:
                        ins = pe.matmul(o[:, w - P:w], k["identb"][:, :], k["mask_qk"][:, :], start=False, stop=True)
                    ins.then_inc(red_ready, 1)

                def max_rows(n, r):
                    for h in range(2):
                        u = len(UNITS) + h
                        pe.wait_ge(max_step, NMAX * n + NMAX)
                        pe.wait_ge(red_done, NUNIT * n + u + 1)
                        apart(pe)
                        o = red_ps[0:HG * TT, u % NR, :].bitcast(BF16)
                        for m in range(2 if h == 0 else 1):
                            ins = pe.transpose(o[:, m * P:(m + 1) * P], mparts[:, 2 * h + m, :], k["identb"][:, :])
                        ins.then_inc(red_ready, 1)

                def scores(n, r, s, heads):
                    J, j = STEPS[s]
                    lo = P if j == 2 * J + 1 else 0
                    if heads[0] == 0:
                        pe.wait_ge(exp_done, NS * n + s + 1)
                    for g in heads:
                        o = st_ps[:, s % 2, g, 0:QB - lo]
                        diag = j >= 2 * J
                        ins = pe.matmul(o, ks[0:SROWS + MROWS, r, g, j * P:(j + 1) * P],
                                        qs[0:SROWS + MROWS, r, g, J * QB + lo:(J + 1) * QB], start=True, stop=not diag)
                        if diag:
                            ins = pe.matmul(o[:, 0:P], k["identb"][:, :], k["mask_kq"][:, :], start=False, stop=True)
                    if heads[-1] == HG - 1:
                        ins.then_inc(st_ready, 1)

                def values(n, r, s):
                    J, j = STEPS[s]
                    lo = P if j == 2 * J + 1 else 0
                    if j == 0:
                        pe.wait_ge(o_done, NJ * n + J + 2)
                    pe.wait_ge(exp_done, NS * n + s + 1 + 2)
                    for g in range(HG):
                        ins = pe.matmul(o_ps[SLOT * g:SLOT * (g + 1), lo:QB], vs[:, r, j, SLOT * g:SLOT * (g + 1)],
                                        probs[:, s % NP, g, 0:QB - lo], start=(j == 0), stop=(s == LAST[J]))
                    ins.then_inc(pv_done, 1)

                def loaded(n, r):
                    if isinstance(n, int):
                        pe.wait_ge(ld[r], LD * (n // R + 1))

                def step(a, b, count=None):
                    if a is not None:
                        pe.wait_ge(ld[a[1]], count)
                    if b is None:
                        for u in range(len(UNITS)):
                            unit(*a, u)
                        return max_rows(*a)
                    n, r = b
                    pe.wait_ge(m_ld, M_LD * n + M_LD + 1)
                    for s in range(NS):
                        units = at_step[s] if a is not None else []
                        scores(n, r, s, (0, 1))
                        for u in units[:1]:
                            unit(*a, u)
                        scores(n, r, s, (2, 3))
                        for u in units[1:2]:
                            unit(*a, u)
                        if s > 0:
                            values(n, r, s - 1)
                        for u in units[2:]:
                            unit(*a, u)
                        if s == MAX_STEP and a is not None:
                            max_rows(*a)
                    values(n, r, NS - 1)

                pe.wait_ge(init_done, 1)
                step((0, 0), None, LD)
                pe.wait_ge(pool_init, 2)
                with pe.Fori(0, NIT // R) as i:
                    for r in range(R):
                        n = R * i + r
                        step((n + 1, (r + 1) % R), (n, r), LD * i + LD * ((r + 1) // R + 1))
                step(None, (NIT - 1, (NIT - 1) % R))

            @block.scalar
            def _(act):
                def output(n, J):
                    act.wait_ge(pv_done, NS * n + LAST[J] + 1 + NP)
                    act.wait_ge(o_st[J % 2], 16 * (NJ // 2 * n + J // 2) + 1)
                    act.copy(o_sb[:, J % 2, :], o_ps).then_inc(o_done, 1)

                def step(a, b):
                    if b is None:
                        return
                    n, r = b
                    for s in range(NS):
                        J, j = STEPS[s]
                        if s - 2 in LAST.values():
                            output(n, STEPS[s - 2][0])
                        w = P if j == 2 * J + 1 else QB
                        act.wait_ge(st_ready, NS * n + s + 1)
                        act.wait_ge(pv_done, NS * n + s + 1)
                        act.activation(probs[:, s % NP, :, 0:w], st_ps[:, s % 2, :, 0:w], ACT.Exp,
                                       scale=DH ** -0.5).then_inc(exp_done, 1)
                    output(n, NJ - 1)

                iterations(act, step)

            @block.vector
            def _(dve):
                dve.memset(ks[SROWS:SROWS + MROWS, 0, :, :], 1.0)
                dve.memset(mxc[:, :, :, :], -3e38).then_inc(init_done, 1)
                dve.wait_ge(init_done, 1)

                def unit(n, u):
                    i, g, c = UNITS[u]
                    w = min(512, P * (i + 1) - 512 * c)
                    dve.wait_ge(red_ready, NUNIT * n + u + 1)
                    dve.tensor_reduce(mxc[:, g, i, c:c + 1], red_ps[:, u % NR, 0:w], AX_X, ALU.max).then_inc(red_done, 1)

                def maxima(n):
                    at = NMAX * n

                    def link(q, ins):
                        ins.then_inc(max_step, 1)
                        dve.wait_ge(max_step, at + q)

                    mp = mparts[:, :, :].rearrange("p m (g i) -> p m g i", g=HG)
                    dve.wait_ge(red_done, NUNIT * n + len(UNITS) + NR)
                    link(1, dve.tensor_reduce(negm[:, :, :], mxc[:, :, :, :], AX_X, ALU.max))
                    link(2, dve.tensor_scalar(negm[:, :, :], negm[:, :, :], -1.0, None, ALU.mult))
                    link(3, dve.tensor_copy(mp[:, 0], negm[:, :, :]))
                    link(4, dve.tensor_tensor(res[:, :, :], negm[:, :, :], mp[:, 0], ALU.subtract))
                    link(5, dve.tensor_copy(mp[:, 1], res[:, :, :]))
                    link(6, dve.tensor_tensor(res[:, :, :], res[:, :, :], mp[:, 1], ALU.subtract))
                    link(7, dve.tensor_copy(mp[:, 2], res[:, :, :]))
                    dve.nop().then_inc(max_step, 2)

                def max_rows(n):
                    dve.wait_ge(m_ld, M_LD * n + 1)
                    for h in range(2):
                        u = len(UNITS) + h
                        w = 2 - h
                        dve.wait_ge(red_ready, NUNIT * n + u + 1)
                        ins = dve.tensor_copy(m_t[:, 2 * h:2 * h + w, :],
                                              red_ps[0:HG * TT, u % NR, :].bitcast(BF16)[:, 0:w * P])
                        ins.then_inc(red_done, 1)
                    dve.wait_ge(red_done, NUNIT * n + NUNIT + NR)
                    dve.nop().then_inc(mt_done, 1)

                def step(a, b):
                    if b is None:
                        for u in range(len(UNITS)):
                            unit(a[0], u)
                        maxima(a[0])
                        return max_rows(a[0])
                    n, r = b
                    for s in range(NS):
                        if a is not None:
                            for u in at_step[s]:
                                unit(a[0], u)
                            if s == SPREAD:
                                maxima(a[0])
                            if s == MAX_STEP:
                                max_rows(a[0])

                iterations(dve, step)


def route(nc, a, d, k, r, ps):
    with ExitStack() as ctx:
        def sb(name, shape, dt=F32):
            return ctx.enter_context(nc.sbuf_tensor(name, shape, dt))

        def sem(name):
            return ctx.enter_context(nc.semaphore("r_" + name))

        o_t = sb("o_t", [P, 2, NG, BLK])
        x_in, x_mid = sb("x_in", [P, BPS, TPB, C]), sb("x_midb", [P, 2, TPB, C])
        rc, yn, y_t = sb("rc", [P, TPB, H]), sb("yn", [P, TPB, C]), sb("y_t", [P, TPB, KC, P])
        stats, mv = sb("stats2", [P, TPB, 6]), sb("mv2", [P, TPB, 2])
        std, rstd = sb("std2", [P, TPB]), sb("rstd2", [P, TPB])
        hn, h2s, h2_t = sb("hn", [P, TPB, C]), sb("h2s", [P, 2, TPB, C]), sb("h2_t", [P, TPB, KC, P])
        lg = sb("lg", [P, TPB, ET])
        top, topi = sb("top", [P, TPB, 8]), sb("topi", [P, TPB, 8], U32)
        o_ld, x_ld = [sem(f"o{j}") for j in range(2)], [sem(f"x{j}") for j in range(BPS)]
        ta_done, rc_step, tb_done, yt_done, out_done = (sem(n) for n in ("ta", "rc", "tb", "yt", "out"))
        norm_step, std_done, hn_done, mod_step, tc_done, ht_done, h2c_done, lg_done, top_step = (
            sem(n) for n in ("norm", "std", "hn", "mod", "tc", "ht", "h2c", "lg", "top"))
        x_st = [sem(f"xs{j}") for j in range(2)]
        pa, pb, pc, pd = ps[:, 0:2, :], ps[:, 2:4, :], ps[:, 4:6, :], ps[:, 6:8, :]
        pb4 = pb.rearrange("p n (j c t) -> p (n j) c t", j=2, c=KC)
        pc4 = pc.rearrange("p n (j c) -> p (n j) c", j=2)
        pd4 = pd.rearrange("p n (j c t) -> p (n j) c t", j=2, c=KC)
        pl = pd[:, 0, 0:TPB * ET].rearrange("p (j e) -> p j e", j=TPB)
        NORM, TOP = 4, 5
        x_v = a["L0_attn_x"].rearrange("b (n j p) c -> b n p j c", p=P, j=TPB)
        m_v = d["x_mid"].rearrange("(b n j p) c -> b n p j c", p=P, j=TPB, n=BPS)

        with nc.Block() as block:
            @block.sync
            def _(sp):
                sp.sem_inc(ta_done, 2 * TPB)
                sp.sem_inc(rc_step, 2 * 2)
                sp.sem_inc(mod_step, 1)
                sp.sem_inc(tc_done, 2)
                sp.sem_inc(h2c_done, 2)
                sp.sem_inc(norm_step, BPS * NORM)
                for s in (yt_done, top_step, x_st[0], x_st[1]):
                    sp.sem_inc(s, 1)

                def load(b, j):
                    par, t = j % 2, BPS * b + j
                    sp.wait_ge(ta_done, TPB * t + TPB)
                    sp.dma_start(o_t[:, par, :, :], d["attn_t"][bass.ds(b, 1), :, :, j * BLK:(j + 1) * BLK].rearrange(
                        "o g p t -> (o p) g t")).then_inc(o_ld[par], 16)
                    sp.wait_ge(norm_step, NORM * t + 1)
                    sp.dma_start(x_in[:, j, :, :], x_v[bass.ds(b, 1), j].rearrange("o p j c -> (o p) j c")).then_inc(x_ld[j], 16)

                def store(b, j):
                    par, t = j % 2, BPS * b + j
                    sp.wait_ge(norm_step, NORM * (t + BPS) + 1)
                    apart(sp)
                    sp.dma_start(m_v[bass.ds(b, 1), j].rearrange("o p j c -> (o p) j c"), x_mid[:, par, :, :]).then_inc(x_st[par], 16)

                staged(sp, (0, load), (2, store))
                for par in range(2):
                    sp.wait_ge(x_st[par], 16 * NB // 2 + 1)

            @block.tensor
            def _(pe):
                def attended(b, j):
                    t, par = BPS * b + j, j % 2
                    pe.wait_ge(o_ld[par], 16 * (2 * b + j // 2 + 1))
                    for n in range(TPB):
                        pe.wait_ge(rc_step, 2 * (TPB * t + n) + 2)
                        for g in range(NG):
                            ins = pe.transpose(pa[:, n % 2, g * P:(g + 1) * P], o_t[:, par, g, n * P:(n + 1) * P], k["ident"][:, :])
                        ins.then_inc(ta_done, 1)

                def turned(b, j):
                    t = BPS * b + j
                    pe.wait_ge(yt_done, t + 1)
                    for n in range(TPB):
                        pe.wait_ge(rc_step, 2 * (TPB * t + n) + 2 + 4)
                        for c in range(KC):
                            ins = pe.transpose(pb4[:, n, c, :], yn[:, n, c * P:(c + 1) * P], k["ident"][:, :])
                    ins.then_inc(tb_done, 1)

                def output(b, j):
                    t = BPS * b + j
                    pe.wait_ge(yt_done, t + 2)
                    pe.wait_ge(norm_step, NORM * (t + BPS - 1) + 1)
                    for n in range(TPB):
                        for c in range(KC):
                            ins = pe.matmul(pc4[:, n, :], y_t[:, n, c, :], k["wc"][:, bass.ds(b, 1), c, :].rearrange("p o n -> p (o n)"),
                                            start=(c == 0), stop=(c == KC - 1))
                    ins.then_inc(out_done, 1)

                def normed(b, j):
                    t = BPS * b + j
                    pe.wait_ge(mod_step, 2 * t + 2 + 1)
                    pe.wait_ge(top_step, TOP * t + 1)
                    for n in range(TPB):
                        for c in range(KC):
                            ins = pe.transpose(pd4[:, n, c, :], h2s[:, j % 2, n, c * P:(c + 1) * P], k["ident"][:, :])
                    ins.then_inc(tc_done, 1)

                def logits(b, j):
                    t = BPS * b + j
                    pe.wait_ge(ht_done, t + 1)
                    for n in range(TPB):
                        for c in range(KC):
                            ins = pe.matmul(pl[:, n, :], h2_t[:, n, c, :], k["gate"][:, c, :], start=(c == 0), stop=(c == KC - 1))
                    ins.then_inc(lg_done, 1)

                staged(pe, (1, output), (0, attended), (3, normed), (0, turned), (3, logits))

            @block.vector
            def _(dve):
                def normalise(b, j):
                    t, par = BPS * b + j, j % 2
                    for n in range(TPB):
                        q = 2 * (TPB * t + n) + 4
                        src = pa[:, n % 2, :].rearrange("p (h s) -> p h s", s=SLOT)
                        dve.wait_ge(ta_done, TPB * t + n + 1 + 2 * TPB)
                        if n == 0:
                            dve.wait_ge(yt_done, t + 1)
                        dve.reciprocal(rc[:, n, :], src[:, :, DH]).then_inc(rc_step, 1)
                        dve.wait_ge(rc_step, q + 1)
                        dve.tensor_tensor(yn[:, n, :].rearrange("p (h s) -> p h s", s=DH), src[:, :, 0:DH],
                                          wide(rc[:, n, :, None], 2, DH), ALU.mult).then_inc(rc_step, 1)

                def residual(b, j):
                    t, par = BPS * b + j, j % 2
                    at = NORM * (t + BPS)
                    dve.wait_ge(out_done, t + 1)
                    dve.wait_ge(x_ld[j], 16 * b + 16)
                    dve.wait_ge(x_st[par], 16 * (2 * b + j // 2) + 1)
                    dve.tensor_tensor(x_mid[:, par, :, :], pc4, x_in[:, j, :, :], ALU.add).then_inc(norm_step, 1)
                    dve.wait_ge(norm_step, at + 1)
                    for n in range(TPB):
                        ins = dve.bn_stats(stats[:, n, :], x_mid[:, par, n, :])
                    ins.then_inc(norm_step, 1)
                    dve.wait_ge(norm_step, at + 2)
                    apart(dve)
                    for n in range(TPB):
                        ins = dve.bn_aggr(mv[:, n, :], stats[:, n, :])
                    ins.then_inc(norm_step, 1)

                def norm(b, j):
                    t, par = BPS * b + j, j % 2
                    at = NORM * (t + BPS)
                    dve.wait_ge(std_done, t + 1)
                    dve.reciprocal(rstd[:, :], std[:, :]).then_inc(norm_step, 1)
                    dve.wait_ge(norm_step, at + 4)
                    dve.wait_ge(mod_step, 2 * t + 1)
                    for n in range(TPB):
                        ins = dve.tensor_scalar(hn[:, n, :], x_mid[:, par, n, :], mv[:, n, 0:1], rstd[:, n:n + 1],
                                                ALU.subtract, ALU.mult)
                    ins.then_inc(hn_done, 1)

                def top2(b, j):
                    t = BPS * b + j
                    at = TOP * t + 1
                    dve.wait_ge(lg_done, t + 1)
                    dve.tensor_tensor(lg[:, :, :], pl, wide(k["bias"][:, None, :], 1, TPB), ALU.add).then_inc(top_step, 1)
                    dve.wait_ge(top_step, at + 1)
                    apart(dve)
                    for n in range(TPB):
                        ins = dve.max(top[:, n, :], lg[:, n, :])
                    ins.then_inc(top_step, 1)
                    dve.wait_ge(top_step, at + 2)
                    apart(dve)
                    for n in range(TPB):
                        ins = dve.max_index(topi[:, n, :], top[:, n, :], lg[:, n, :])
                    ins.then_inc(top_step, 1)
                    dve.wait_ge(top_step, at + 3)
                    dve.tensor_copy(r["top2"][:, bass.ds(TPB * t, TPB), :], top[:, :, 0:2]).then_inc(top_step, 1)
                    dve.tensor_copy(r["idx2"][:, bass.ds(TPB * t, TPB), :], topi[:, :, 0:2]).then_inc(top_step, 1)
                    dve.wait_ge(top_step, at + 5)

                staged(dve, (0, normalise), (1, residual), (1, norm), (3, top2))

            @block.scalar
            def _(act):
                def turned(b, j):
                    t = BPS * b + j
                    act.wait_ge(tb_done, t + 1)
                    if not isinstance(b, int) or b + j > 0:
                        act.wait_ge(out_done, t)
                    act.copy(y_t[:, :, :, :], pb4).then_inc(yt_done, 1)

                def deviation(b, j):
                    t = BPS * b + j
                    act.wait_ge(norm_step, NORM * (t + BPS) + 3)
                    act.activation(std[:, :], mv[:, :, 1], ACT.Sqrt, bias=k["eps"][:, :]).then_inc(std_done, 1)

                def keep(b, j):
                    t = BPS * b + j
                    act.wait_ge(mod_step, 2 * t + 2 + 1)
                    act.copy(r["h2"][:, bass.ds(TPB * t, TPB), :], h2s[:, j % 2, :, :]).then_inc(h2c_done, 1)

                def normed(b, j):
                    t = BPS * b + j
                    act.wait_ge(tc_done, t + 1 + 2)
                    act.copy(h2_t[:, :, :, :], pd4).then_inc(ht_done, 1)

                staged(act, (3, normed), (0, turned), (1, deviation), (2, keep))

            @block.gpsimd
            def _(pool):
                def modulate(b, j):
                    t, o = BPS * b + j, h2s[:, j % 2, :, :]
                    pool.wait_ge(hn_done, t + 1)
                    pool.wait_ge(tc_done, t + 1)
                    pool.wait_ge(h2c_done, t + 1)
                    apart(pool)
                    pool.tensor_tensor(o, hn[:, :, :], wide(k["sbc"][:, bass.ds(b, 1), 1, :], 1, TPB), ALU.mult).then_inc(mod_step, 1)
                    pool.wait_ge(mod_step, 2 * t + 1 + 1)
                    apart(pool)
                    pool.tensor_tensor(o, o, wide(k["sbc"][:, bass.ds(b, 1), 0, :], 1, TPB), ALU.add).then_inc(mod_step, 1)

                staged(pool, (0, modulate))


def place(nc, a, d, k, r, w, ps):
    with ExitStack() as ctx:
        def sb(name, shape, dt=F32):
            return ctx.enter_context(nc.sbuf_tensor(name, shape, dt))

        def sem(name):
            return ctx.enter_context(nc.semaphore("l_" + name))

        consts = {n: sb(n, s) for n, s in {"tri": [P, P], "ones": [P, P], "iota_e": [P, ET], "iota_t": [P, NSLOT_T + 2],
                                           "spare": [P, NT]}.items()}
        idxf, oh, ohs = sb("idxf", [P, NT, 2]), sb("oh", [P, 2, NT, ET]), sb("ohs", [P, NT, E])
        cum, rank = sb("cum", [P, 2, NT, E]), sb("rank", [P, NT, E])
        cnt, cnt_i, base, tend = sb("cnt", [P, E]), sb("cnt_i", [P, E], I32), sb("base", [P, E]), sb("tend", [P, E])
        sel, zero, posf = sb("sel", [P, NT, E]), sb("zerof", [P, 2, NT]), sb("posf", [P, NT])
        dif, wtmp = sb("dif", [P, NT]), sb("wtmp", [P, NT])
        cmp, eidf = sb("cmp", [P, NSLOT_T + 2, E]), sb("eidf", [P, NSLOT_T + 2])
        w_in = sb("w_in", [P, 2, FC * C])
        c_ld, step, w_dif, w_sig, cnt_mm, pos_done, scat, tr_done, tr_copy = (
            sem(n) for n in ("c", "step", "dif", "sig", "cnt", "pos", "scat", "tr", "trc"))
        w_ld = [sem(f"w{j}") for j in range(2)]
        NW = 2 * E

        with nc.Block() as block:
            @block.sync
            def _(sp):
                sp.sem_inc(tr_done, 4)
                sp.sem_inc(tr_copy, 2)
                for n in consts:
                    sp.dma_start(consts[n][:, :], a[n]).then_inc(c_ld, 16)
                w1_v = a["L0_ffn_w1"].rearrange("e (f p) c -> e p f c", p=P)
                w2_v = a["L0_ffn_w2"].rearrange("e (c p) f -> e p c f", p=P)
                with sp.Fori(0, E) as e:
                    sp.wait_ge(tr_done, 4 * e + 2)
                    sp.dma_start(w_in[:, 0, :].rearrange("p (f c) -> p f c", f=FC),
                                 w1_v[bass.ds(e, 1)].rearrange("o p f c -> (o p) f c")).then_inc(w_ld[0], 16)
                    sp.wait_ge(tr_done, 4 * e + 4)
                    sp.dma_start(w_in[:, 1, :].rearrange("p (c f) -> p c f", c=KC),
                                 w2_v[bass.ds(e, 1)].rearrange("o p c f -> (o p) c f")).then_inc(w_ld[1], 16)

            @block.tensor
            def _(pe):
                pe.wait_ge(c_ld, 16 * len(consts))
                pe.wait_ge(step, 5)
                pe.matmul(ps[:, 0, :], consts["tri"][:, :], ohs[:, :, :].rearrange("p t e -> p (t e)"), start=True, stop=True)
                pe.matmul(ps[:, 1, :], consts["ones"][:, :], ohs[:, :, :].rearrange("p t e -> p (t e)"),
                          start=True, stop=True).then_inc(cnt_mm, 1)
                with pe.Fori(0, E) as e:
                    for half in range(4):
                        m, h = half // 2, half % 2
                        if h == 0:
                            pe.wait_ge(w_ld[m], 16 * e + 16)
                        pe.wait_ge(tr_copy, 4 * e + half + 1)
                        for q in range(4):
                            at = (q * KC + h) * P if m == 0 else ((q % 2) * FC + 2 * h + q // 2) * P
                            ins = pe.transpose(ps[:, 2 + half % 2, q * P:(q + 1) * P], w_in[:, m, at:at + P], k["ident"][:, :])
                        ins.then_inc(tr_done, 1)

            @block.scalar
            def _(act):
                act.wait_ge(w_dif, 1)
                act.activation(r["w12"][:, :, 0], dif[:, :], ACT.Sigmoid)
                act.activation(r["w12"][:, :, 1], dif[:, :], ACT.Sigmoid, scale=-1.0).then_inc(w_sig, 1)
                with act.Fori(0, E) as e:
                    for half in range(4):
                        m, h = half // 2, half % 2
                        act.wait_ge(tr_done, 4 * e + half + 1 + 4)
                        src = ps[:, 2 + half % 2, :]
                        if m == 0:
                            dst = w["w1t"][:, bass.ds(e, 1), h, :].rearrange("p o f -> p (o f)")
                        else:
                            dst = w["w2t"][:, bass.ds(e, 1), 2 * h:2 * h + 2, :].rearrange("p o f c -> p (o f c)")
                        act.copy(dst, src).then_inc(tr_copy, 1)

            @block.vector
            def _(dve):
                s = Steps(dve, step)
                dve.wait_ge(c_ld, 16 * len(consts))
                dve.tensor_tensor(dif[:, :], r["top2"][:, :, 0], r["top2"][:, :, 1], ALU.subtract).then_inc(w_dif, 1)
                s.link(dve.tensor_copy(idxf[:, :, :], r["idx2"][:, :, :]))
                for c in range(2):
                    s.link(dve.tensor_tensor(oh[:, c, :, :], wide(idxf[:, :, c:c + 1], 2, ET),
                                             wide(consts["iota_e"][:, None, :], 1, NT), ALU.is_equal))
                s.link(dve.tensor_tensor(ohs[:, :, :], oh[:, 0, :, 0:E], oh[:, 1, :, 0:E], ALU.add))
                s.link(dve.memset(base[:, :], 0.0))
                for c in range(2):
                    s.link(dve.tensor_reduce(zero[:, c, :], oh[:, c, :, E:ET], AX_X, ALU.add))
                dve.wait_ge(w_sig, 1)
                s.link(dve.tensor_tensor(r["wz"][:, :], zero[:, 0, :], r["w12"][:, :, 0], ALU.mult))
                s.link(dve.tensor_tensor(wtmp[:, :], zero[:, 1, :], r["w12"][:, :, 1], ALU.mult))
                s.link(dve.tensor_tensor(r["wz"][:, :], r["wz"][:, :], wtmp[:, :], ALU.add))
                dve.wait_ge(cnt_mm, 1)
                s.link(dve.tensor_copy(rank[:, :, :], ps[:, 0, :]))
                s.link(dve.tensor_copy(cum[:, 0, :, :], ps[:, 1, :]))
                s.link(dve.tensor_tensor(rank[:, :, :], rank[:, :, :], cum[:, 0, :, :], ALU.subtract))
                src, sh = 0, 1
                while sh < NT:
                    s.mark(dve.tensor_copy(cum[:, 1 - src, 0:sh, :], cum[:, src, 0:sh, :]))
                    s.link(dve.tensor_tensor(cum[:, 1 - src, sh:, :], cum[:, src, sh:, :], cum[:, src, 0:NT - sh, :], ALU.add))
                    src, sh = 1 - src, 2 * sh
                s.link(dve.tensor_tensor(rank[:, :, :], rank[:, :, :], cum[:, src, :, :], ALU.add))
                s.link(dve.tensor_scalar(cnt[:, :], cum[:, src, NT - 1, :], float(P - 1), None, ALU.add))
                s.link(dve.tensor_copy(cnt_i[:, :], cnt[:, :]))
                s.link(dve.tensor_scalar(cnt_i[:, :], cnt_i[:, :], 7, None, ALU.arith_shift_right))
                s.link(dve.tensor_copy(cnt[:, :], cnt_i[:, :]))
                for e in range(1, E):
                    s.link(dve.tensor_tensor(base[:, e:e + 1], base[:, e - 1:e], cnt[:, e - 1:e], ALU.add))
                s.link(dve.tensor_tensor(tend[:, :], base[:, :], cnt[:, :], ALU.add))
                s.link(dve.tensor_scalar(cnt[:, 0:1], tend[:, E - 1:E], 1.0, None, ALU.add))
                s.link(dve.tensor_copy(w["npair"][:, :], cnt[:, 0:1]))
                s.link(dve.tensor_scalar(w["npair"][:, :], w["npair"][:, :], 1, None, ALU.arith_shift_right))
                s.link(dve.tensor_scalar(base[:, :], base[:, :], float(P), None, ALU.mult))
                s.link(dve.tensor_tensor(rank[:, :, :], rank[:, :, :], wide(base[:, None, :], 1, NT), ALU.add))
                for c in range(2):
                    s.link(dve.tensor_tensor(sel[:, :, :], rank[:, :, :], oh[:, c, :, 0:E], ALU.mult))
                    s.link(dve.tensor_reduce(posf[:, :], sel[:, :, :], AX_X, ALU.add))
                    s.link(dve.scalar_tensor_tensor(wtmp[:, :], consts["spare"][:, :], float(c), zero[:, c, :], ALU.add, ALU.mult))
                    s.link(dve.tensor_tensor(posf[:, :], posf[:, :], wtmp[:, :], ALU.add))
                    s.link(dve.tensor_copy(r["pos"][c][:, :], posf[:, :]))
                    dve.nop().then_inc(pos_done, 1)
                    s.link(dve.tensor_scalar(posf[:, :], posf[:, :], float(ZROW), None, ALU.min))
                    s.link(dve.tensor_copy(r["gpos"][c][:, :], posf[:, :]))
                s.link(dve.tensor_tensor(cmp[:, :, :], wide(tend[:, None, :], 1, NSLOT_T + 2),
                                         wide(consts["iota_t"][:, :, None], 2, E), ALU.is_le))
                s.link(dve.tensor_reduce(eidf[:, :], cmp[:, :, :], AX_X, ALU.add))
                s.link(dve.tensor_scalar(eidf[:, :], eidf[:, :], float(E - 1), None, ALU.min))
                s.link(dve.tensor_copy(w["eid"][:, :], eidf[:, :]))

            @block.gpsimd
            def _(pool):
                for c in range(2):
                    pool.wait_ge(pos_done, c + 1)
                    for t in range(NT):
                        pool.indirect_dma_start(d["slot_x"][:, :], bass.IndirectOffsetOnAxis(ap=r["pos"][c][:, t:t + 1], axis=0),
                                                r["h2"][:, t, :], None).then_inc(scat, 16)
                pool.wait_ge(scat, 16 * 2 * NT)


def experts(nc, d, k, w, ps):
    with ExitStack() as ctx:
        def sb(name, shape, dt=F32):
            return ctx.enter_context(nc.sbuf_tensor(name, shape, dt))

        def sem(name):
            return ctx.enter_context(nc.semaphore("e_" + name))

        xs, ys = sb("xs", [P, 2, C]), sb("ys", [P, 2, C])
        x_t, h_t = sb("x_t", [P, KC, P]), sb("hid_t", [P, 2, FC, P])
        w1_at = sb("w1_at", [P, 2, KC, F])
        x_ld, y_st = [sem(f"x{j}") for j in range(2)], [sem(f"y{j}") for j in range(2)]
        tx_done, xt_done, w1_done, up_done, silu_done, down_done, y_done = (
            sem(n) for n in ("tx", "xt", "w1", "up", "silu", "down", "y"))
        px, ph, py = ps[:, 0, :], ps[:, 1:3, :], ps[:, 3:5, :]
        NPAIR = NSLOT_T // 2
        xv = d["slot_x"][0:NSLOT + 2 * P, :].rearrange("(n p) c -> n p c", p=P)
        yv = d["slot_y"][0:NSLOT, :].rearrange("(n p) c -> n p c", p=P)

        def pairs(eng, body):
            used = eng.value_load(w["npair"][0:1, 0:1], min_val=0, max_val=NPAIR)
            with eng.Fori(0, NPAIR) as i:
                with eng.If(i < used):
                    for q in range(2):
                        body(2 * i + q, q, i)
            return used

        with nc.Block() as block:
            @block.sync
            def _(sp):
                sp.sem_inc(y_done, 2)
                for q in range(2):
                    sp.sem_inc(y_st[q], 1)

                def load(t, q):
                    sp.dma_start(xs[:, q, :], xv[bass.ds(t, 1)].rearrange("o p c -> (o p) c")).then_inc(x_ld[q], 16)

                def body(t, q, i):
                    sp.wait_ge(tx_done, t + 1)
                    load(t + 2, q)

                load(0, 0)
                load(1, 1)
                pairs(sp, body)

            @block.tensor
            def _(pe):
                def turn_x(t, q, i):
                    pe.wait_ge(x_ld[q], 16 * i + 16)
                    for c in range(KC):
                        ins = pe.transpose(px[:, c * P:(c + 1) * P], xs[:, q, c * P:(c + 1) * P], k["ident"][:, :])
                    ins.then_inc(tx_done, 1)

                def up(t, q):
                    pe.wait_ge(xt_done, t + 1)
                    pe.wait_ge(w1_done, t + 1)
                    for f in range(FC):
                        for c in range(KC):
                            ins = pe.matmul(ph[:, q, f * P:(f + 1) * P], w1_at[:, q, c, f * P:(f + 1) * P], x_t[:, c, :],
                                            start=(c == 0), stop=(c == KC - 1))
                    ins.then_inc(up_done, 1)

                def down(t, q):
                    e = pe.value_load(w["eid"][0:1, bass.ds(t, 1)], min_val=0, max_val=E - 1)
                    pe.wait_ge(silu_done, t + 1)
                    pe.wait_ge(y_done, t + 1)
                    for f in range(FC):
                        ins = pe.matmul(py[:, q, 0:C], h_t[:, q, f, :], w["w2t"][:, bass.ds(e, 1), f, :].rearrange("p o c -> p (o c)"),
                                        start=(f == 0), stop=(f == FC - 1))
                    ins.then_inc(down_done, 1)

                def body(t, q, i):
                    up(t + 1, 1 - q)
                    turn_x(t + 2, q, i + 1)
                    down(t, q)

                turn_x(0, 0, 0)
                up(0, 0)
                turn_x(1, 1, 0)
                pairs(pe, body)

            @block.scalar
            def _(act):
                def silu(t, q):
                    act.wait_ge(up_done, t + 1)
                    act.activation(h_t[:, q, :, :], ph[:, q, :], ACT.Silu).then_inc(silu_done, 1)

                def body(t, q, i):
                    silu(t + 1, 1 - q)
                    act.wait_ge(y_done, t + 1 + 2)
                    act.dma_start(yv[bass.ds(t, 1)].rearrange("o p c -> (o p) c"), ys[:, q, :]).then_inc(y_st[q], 16)

                silu(0, 0)
                used = pairs(act, body)
                for q in range(2):
                    act.wait_ge(y_st[q], 16 * used + 1)
                apart(act)

            @block.vector
            def _(dve):
                def copy_x(t):
                    dve.wait_ge(tx_done, t + 1)
                    dve.tensor_copy(x_t[:, :, :], px[:, 0:C]).then_inc(xt_done, 1)

                def copy_w1(t, q):
                    e = dve.value_load(w["eid"][0:1, bass.ds(t, 1)], min_val=0, max_val=E - 1)
                    dve.tensor_copy(w1_at[:, q, :, :], w["w1t"][:, bass.ds(e, 1), :, :].rearrange("p o c f -> p (o c) f")).then_inc(w1_done, 1)

                def body(t, q, i):
                    copy_x(t + 2)
                    copy_w1(t + 2, q)
                    dve.wait_ge(down_done, t + 1)
                    dve.wait_ge(y_st[q], 16 * i + 1)
                    dve.tensor_copy(ys[:, q, :], py[:, q, 0:C]).then_inc(y_done, 1)

                for t in range(2):
                    copy_w1(t, t)
                    copy_x(t)
                pairs(dve, body)


def combine(nc, d, k, r, out):
    with ExitStack() as ctx:
        def sb(name, shape, dt=F32):
            return ctx.enter_context(nc.sbuf_tensor(name, shape, dt))

        def sem(name):
            return ctx.enter_context(nc.semaphore("c_" + name))

        R = 4
        G = 2 * R
        y = sb("y_in", [P, 2, G, C])
        xm, acc = sb("xm", [P, 2, R, C]), sb("acc", [P, 2, R, C])
        g_ld = [[sem(f"g{c}{q}") for q in range(G)] for c in range(2)]
        x_ld, o_st = [sem(f"x{q}") for q in range(2)], [sem(f"o{q}") for q in range(2)]
        used, step, done = sem("used"), sem("step"), sem("done")
        NGRP = NT // R
        ACC = 3
        xv = d["x_mid"].rearrange("(n j p) c -> n p j c", p=P, j=R)
        ov = out.rearrange("b (n j p) c -> (b n) p j c", p=P, j=R)

        with nc.Block() as block:
            @block.gpsimd
            def _(pool):
                for t in range(NT):
                    if t >= G:
                        pool.wait_ge(used, t - G + 1)
                    for c in range(2):
                        pool.indirect_dma_start(y[:, c, t % G, :], None, d["slot_y"][:, :],
                                                bass.IndirectOffsetOnAxis(ap=r["gpos"][c][:, t:t + 1], axis=0)).then_inc(g_ld[c][t % G], 16)

            @block.sync
            def _(sp):
                def load(n, q):
                    sp.dma_start(xm[:, q, :, :], xv[bass.ds(n, 1)].rearrange("o p j c -> (o p) j c")).then_inc(x_ld[q], 16)

                def store(n, q):
                    sp.wait_ge(done, n + 1)
                    sp.dma_start(ov[bass.ds(n, 1)].rearrange("o p j c -> (o p) j c"), acc[:, q, :, :]).then_inc(o_st[q], 16)

                for q in range(2):
                    sp.sem_inc(o_st[q], 1)
                    load(q, q)
                with sp.Fori(0, NGRP // 2 - 1) as i:
                    for q in range(2):
                        store(2 * i + q, q)
                        load(2 * i + q + 2, q)
                for q in range(2):
                    store(NGRP - 2 + q, q)
                for q in range(2):
                    sp.wait_ge(o_st[q], 16 * NGRP // 2 + 1)

            @block.vector
            def _(dve):
                GPS = NGRP // B
                with dve.Fori(0, B) as b:
                    for j in range(GPS):
                        g, q, i = GPS * b + j, j % 2, GPS // 2 * b + j // 2
                        at = (ACC * R + 1) * g
                        dve.wait_ge(o_st[q], 16 * i + 1)
                        for n in range(R):
                            m = R * q + n
                            dve.wait_ge(g_ld[0][m], 16 * i + 16)
                            dve.tensor_scalar(acc[:, q, n, :], y[:, 0, m, :], r["w12"][:, bass.ds(R * g + n, 1), 0], None,
                                              ALU.mult).then_inc(step, 1)
                        for n in range(R):
                            o, m = acc[:, q, n, :], R * q + n
                            dve.wait_ge(step, at + n + 1)
                            dve.wait_ge(g_ld[1][m], 16 * i + 16)
                            dve.scalar_tensor_tensor(o, y[:, 1, m, :], r["w12"][:, bass.ds(R * g + n, 1), 1], o, ALU.mult,
                                                     ALU.add).then_inc(step, 1)
                        for n in range(R):
                            o = acc[:, q, n, :]
                            dve.wait_ge(step, at + R + n + 1)
                            dve.nop().then_inc(used, 1)
                            dve.scalar_tensor_tensor(o, r["h2"][:, bass.ds(R * g + n, 1), :].rearrange("p o c -> p (o c)"),
                                                     r["wz"][:, bass.ds(R * g + n, 1)], o, ALU.mult, ALU.add).then_inc(step, 1)
                        dve.wait_ge(step, at + ACC * R)
                        gb = wide(k["gb"][:, bass.ds(b, 1), :], 1, R)
                        dve.tensor_tensor(acc[:, q, :, :], acc[:, q, :, :], gb, ALU.mult).then_inc(step, 1)
                        dve.wait_ge(step, at + ACC * R + 1)
                        dve.wait_ge(x_ld[q], 16 * i + 16)
                        dve.tensor_tensor(acc[:, q, :, :], acc[:, q, :, :], xm[:, q, :, :], ALU.add).then_inc(done, 1)


_INS = ["L0_attn_x", "L0_attn_Wq_down", "L0_attn_Wk_down", "L0_attn_Wv_down", "L0_attn_Wq_up_c", "L0_attn_Wq_up_e",
        "L0_attn_Wk_up_c", "L0_attn_Wk_up_e", "L0_attn_Wv_up", "L0_attn_Wc", "L0_ffn_gate_w", "L0_ffn_expert_bias",
        "L0_ffn_w1", "L0_ffn_w2", "L0_c", "L0_wmod"]


def constants():
    p = np.arange(P)
    eye = np.eye(P, dtype=np.float32)
    above = np.where(p[None, :] > p[:, None], np.float32(-BIG), np.float32(0))
    half = DH // 2
    inv = np.float32(1.0) / np.float32(10000.0) ** (np.arange(0, half, 2, dtype=np.float32) / np.float32(half))
    ang = np.arange(T, dtype=np.float32)[:, None] * inv[None, :].astype(np.float32)
    ang = np.concatenate([ang, ang], axis=1).astype(np.float32)
    cos = np.ones((T, DH), np.float32)
    sin = np.zeros((T, DH), np.float32)
    cos[:, half:] = np.cos(ang)
    sin[:, half:] = np.sin(ang) * np.where(np.arange(half) % 2 == 0, -1, 1).astype(np.float32)
    return {
        "ident": eye, "mask_qk": above, "mask_kq": above.T.copy(),
        "cos": np.tile(cos.T, (P // DH, 1)).copy(), "sin": np.tile(sin.T, (P // DH, 1)).copy(),
        "tri": (p[:, None] < p[None, :]).astype(np.float32), "ones": np.ones((P, P), np.float32),
        "iota_e": np.tile(np.arange(ET, dtype=np.float32), (P, 1)),
        "iota_t": np.tile(np.arange(NSLOT_T + 2, dtype=np.float32), (P, 1)),
        "spare": (NSLOT + 2 * P + 2 * (P * np.arange(NT)[None, :] + p[:, None])).astype(np.float32),
    }


def kernel(**inputs):
    import concourse.bacc as _bacc
    from concourse.bass_utils import run_bass_kernel_spmd as _run

    nc = _bacc.Bacc("TRN2", target_bir_lowering=False, num_devices=1)
    arrays, args = {}, {}
    given = {n: np.ascontiguousarray(inputs[n]) for n in _INS}
    for name, x in {**given, **constants()}.items():
        arrays[f"in_{name}"] = x
        args[name] = nc.dram_tensor(f"in_{name}", x.shape, mybir.dt.from_np(x.dtype), kind="ExternalInput").ap()
    out = nc.dram_tensor("out_0", (B, T, C), F32, kind="ExternalOutput").ap()
    build(nc, args, out)
    r = _run(nc, [arrays], core_ids=[0])
    return r.results[0]["out_0"]
```
